# Optimizing a Trainium2 kernel written in Bass

```python
import numpy as np
import jax
import jax.numpy as jnp

def _softmax(x, axis=-1):
    return jax.nn.softmax(x, axis=axis)

def _gelu(x):
    return jax.nn.gelu(x, approximate=True)

def _silu(x):
    return jax.nn.silu(x)

def _sigmoid(x):
    return jax.nn.sigmoid(x)

def _layernorm(x, axis=-1, eps=1e-05):
    m = jnp.mean(x, axis=axis, keepdims=True)
    v = jnp.var(x, axis=axis, keepdims=True)
    return (x - m) / jnp.sqrt(v + eps)

def _scatter_add(tgt, idx, src, axis=0):
    return tgt.at[idx].add(src)

def _segment_sum(src, seg, n):
    return jax.ops.segment_sum(src, seg, n)
kernel_name = 'mk_cond_seq_d2_seqx_r8_41e811'

def setup_inputs(seed: int=0):
    np.random.seed(seed)
    _w = jnp.asarray

    def _rec_inputs():
        import jax
        import jax.numpy as jnp
        _rk = jax.random.key(seed)
        x = 7.22e-05 + 1 * jax.random.normal(jax.random.fold_in(_rk, 1), (8, 128, 256), jnp.float32)
        _lenS = 128 - jax.random.randint(jax.random.fold_in(_rk, 7), (8,), 0, max(1, 128 // 4) + 1, jnp.int32)
        _lenS2 = 128 - jax.random.randint(jax.random.fold_in(_rk, 8), (8,), 0, max(1, 128 // 4) + 1, jnp.int32)
        cond_2048 = 0.0061147 + 1.02565 * jax.random.normal(jax.random.fold_in(_rk, 11), (8, 256), jnp.float32)
        pos_BxS = jnp.broadcast_to(jnp.arange(128, dtype=jnp.int32), (8, 128))
        _validS = jnp.arange(128)[None, :] < _lenS[:, None]
        _validS2 = jnp.arange(128)[None, :] < _lenS2[:, None]
        _causal = jnp.tril(jnp.ones((128, 128), dtype=bool))
        mask_1x1xSxS_ff0 = jnp.where(jnp.ones((1, 1, 128, 128), dtype=bool), 0.0, -1000000000.0).astype(jnp.float32)
        return (x, cond_2048, pos_BxS, mask_1x1xSxS_ff0)
    x, cond_2048, pos_BxS, mask_1x1xSxS_ff0 = _rec_inputs()

    def _L0_cond_setup():
        import jax, jax.numpy as jnp
        import numpy as np
        B, L, C, H = (2, 256, 256, 16)
        COND = 256
        HID = 4 * C
        LN_EPS = 1e-06

        def _ln(x):
            m = jnp.mean(x, axis=-1, keepdims=True)
            v = jnp.mean((x - m) ** 2, axis=-1, keepdims=True)
            return (x - m) / jnp.sqrt(v + LN_EPS)

        def _gelu_tanh(u):
            c = np.sqrt(2.0 / np.pi).astype(np.float32)
            return 0.5 * u * (1.0 + jnp.tanh(c * (u + 0.044715 * u ** 3)))
        key = jax.random.key(seed)
        ks = jax.random.split(key, 8)
        s = 0.02
        return {'x': jax.random.normal(ks[0], (B, L, C), jnp.float32), 'cond_BD': jax.random.normal(ks[1], (B, COND), jnp.float32), 'attn_bias': jnp.zeros((1, 1, L, L), jnp.float32), 'Wqkv': jax.random.normal(ks[2], (3 * C, C), jnp.float32) * s, 'q_bias': jnp.zeros((C,), jnp.float32), 'v_bias': jnp.zeros((C,), jnp.float32), 'scale_mul_log': jnp.full((1, H, 1, 1), np.log(4.0), jnp.float32), 'Wproj': jax.random.normal(ks[3], (C, C), jnp.float32) * s, 'bproj': jnp.zeros((C,), jnp.float32), 'Wada': jax.random.normal(ks[4], (6 * C, COND), jnp.float32) * s, 'bada': jnp.zeros((6 * C,), jnp.float32), 'Wfc1': jax.random.normal(ks[5], (HID, C), jnp.float32) * s, 'bfc1': jnp.zeros((HID,), jnp.float32), 'Wfc2': jax.random.normal(ks[6], (C, HID), jnp.float32) * s, 'bfc2': jnp.zeros((C,), jnp.float32)}
    _L0_cond_all = _L0_cond_setup()
    _L0_cond_in = {k: v for k, v in _L0_cond_all.items() if k in ('Wqkv', 'q_bias', 'v_bias', 'scale_mul_log', 'Wproj', 'bproj', 'Wada', 'bada', 'Wfc1', 'bfc1', 'Wfc2', 'bfc2')}
    del _L0_cond_all

    def _L1_cond_setup():
        import jax, jax.numpy as jnp
        import numpy as np
        HIDDEN, NQ, NKV, HD, INTER = (256, 8, 1, 32, 1024)
        B, S = (4, 256)
        EPS = 1e-06
        ROPE_BASE = 10000.0

        def ada_rms(x, t, w, tw):
            n = x * jax.lax.rsqrt(jnp.mean(jnp.square(x), axis=-1, keepdims=True) + EPS)
            scale = t @ tw.T
            return n * (w * (1.0 + scale))[:, None, :]

        def apply_rope(x, pos_ids):
            half = HD // 2
            inv_freq = 1.0 / ROPE_BASE ** (jnp.arange(0, HD, 2, dtype=jnp.float32) / HD)
            ang = pos_ids.astype(jnp.float32)[:, :, None] * inv_freq
            cos = jnp.concatenate([jnp.cos(ang), jnp.cos(ang)], axis=-1)[:, None]
            sin = jnp.concatenate([jnp.sin(ang), jnp.sin(ang)], axis=-1)[:, None]
            x1, x2 = (x[..., :half], x[..., half:])
            rot = jnp.concatenate([-x2, x1], axis=-1)
            return x * cos + rot * sin
        key = jax.random.key(seed)
        ks = jax.random.split(key, 12)
        f32 = jnp.float32
        inp = {'x': jax.random.normal(ks[0], (B, S, HIDDEN), f32), 'pos_ids': jnp.broadcast_to(jnp.arange(S, dtype=jnp.int32), (B, S)), 'time_emb': jax.random.normal(ks[1], (B, HIDDEN), f32), 'ln1_w': jnp.ones((HIDDEN,), f32), 'ln1_tw': jax.random.normal(ks[2], (HIDDEN, HIDDEN), f32) * 0.02, 'ln2_w': jnp.ones((HIDDEN,), f32), 'ln2_tw': jax.random.normal(ks[3], (HIDDEN, HIDDEN), f32) * 0.02, 'Wq': jax.random.normal(ks[4], (NQ * HD, HIDDEN), f32) * 0.02, 'Wk': jax.random.normal(ks[5], (NKV * HD, HIDDEN), f32) * 0.02, 'Wv': jax.random.normal(ks[6], (NKV * HD, HIDDEN), f32) * 0.02, 'Wo': jax.random.normal(ks[7], (HIDDEN, NQ * HD), f32) * 0.02, 'Wg': jax.random.normal(ks[8], (INTER, HIDDEN), f32) * 0.02, 'Wu': jax.random.normal(ks[9], (INTER, HIDDEN), f32) * 0.02, 'Wd': jax.random.normal(ks[10], (HIDDEN, INTER), f32) * 0.02}
        return inp
    _L1_cond_all = _L1_cond_setup()
    _L1_cond_in = {k: v for k, v in _L1_cond_all.items() if k in ('ln1_w', 'ln1_tw', 'ln2_w', 'ln2_tw', 'Wq', 'Wk', 'Wv', 'Wo', 'Wg', 'Wu', 'Wd')}
    del _L1_cond_all
    return {'x': x, 'cond_2048': cond_2048, 'pos_BxS': pos_BxS, 'mask_1x1xSxS_ff0': mask_1x1xSxS_ff0, 'L0_cond_Wqkv': _L0_cond_in['Wqkv'], 'L0_cond_q_bias': _L0_cond_in['q_bias'], 'L0_cond_v_bias': _L0_cond_in['v_bias'], 'L0_cond_scale_mul_log': _L0_cond_in['scale_mul_log'], 'L0_cond_Wproj': _L0_cond_in['Wproj'], 'L0_cond_bproj': _L0_cond_in['bproj'], 'L0_cond_Wada': _L0_cond_in['Wada'], 'L0_cond_bada': _L0_cond_in['bada'], 'L0_cond_Wfc1': _L0_cond_in['Wfc1'], 'L0_cond_bfc1': _L0_cond_in['bfc1'], 'L0_cond_Wfc2': _L0_cond_in['Wfc2'], 'L0_cond_bfc2': _L0_cond_in['bfc2'], 'L1_cond_ln1_w': _L1_cond_in['ln1_w'], 'L1_cond_ln1_tw': _L1_cond_in['ln1_tw'], 'L1_cond_ln2_w': _L1_cond_in['ln2_w'], 'L1_cond_ln2_tw': _L1_cond_in['ln2_tw'], 'L1_cond_Wq': _L1_cond_in['Wq'], 'L1_cond_Wk': _L1_cond_in['Wk'], 'L1_cond_Wv': _L1_cond_in['Wv'], 'L1_cond_Wo': _L1_cond_in['Wo'], 'L1_cond_Wg': _L1_cond_in['Wg'], 'L1_cond_Wu': _L1_cond_in['Wu'], 'L1_cond_Wd': _L1_cond_in['Wd']}

def reference(x, cond_2048, pos_BxS, mask_1x1xSxS_ff0, L0_cond_Wqkv, L0_cond_q_bias, L0_cond_v_bias, L0_cond_scale_mul_log, L0_cond_Wproj, L0_cond_bproj, L0_cond_Wada, L0_cond_bada, L0_cond_Wfc1, L0_cond_bfc1, L0_cond_Wfc2, L0_cond_bfc2, L1_cond_ln1_w, L1_cond_ln1_tw, L1_cond_ln2_w, L1_cond_ln2_tw, L1_cond_Wq, L1_cond_Wk, L1_cond_Wv, L1_cond_Wo, L1_cond_Wg, L1_cond_Wu, L1_cond_Wd):
    import jax
    import jax.numpy as jnp

    def _L0_cond_ref(x, cond_BD, attn_bias, Wqkv, q_bias, v_bias, scale_mul_log, Wproj, bproj, Wada, bada, Wfc1, bfc1, Wfc2, bfc2):
        import jax, jax.numpy as jnp
        import numpy as np
        B, L, C, H = (2, 256, 256, 16)
        COND = 256
        HID = 4 * C
        LN_EPS = 1e-06

        def _ln(x):
            m = jnp.mean(x, axis=-1, keepdims=True)
            v = jnp.mean((x - m) ** 2, axis=-1, keepdims=True)
            return (x - m) / jnp.sqrt(v + LN_EPS)

        def _gelu_tanh(u):
            c = np.sqrt(2.0 / np.pi).astype(np.float32)
            return 0.5 * u * (1.0 + jnp.tanh(c * (u + 0.044715 * u ** 3)))
        Bs, Lx, Cx = x.shape
        D = Cx // H
        ada = (jax.nn.silu(cond_BD) @ Wada.T + bada).reshape(Bs, 1, 6, Cx)
        gamma1, gamma2, scale1, scale2, shift1, shift2 = [ada[:, :, i, :] for i in range(6)]

        def attn(xin):
            qkv_bias = jnp.concatenate([q_bias, jnp.zeros_like(q_bias), v_bias])
            qkv = (xin @ Wqkv.T + qkv_bias).reshape(Bs, Lx, 3, H, D)
            qkv = jnp.transpose(qkv, (2, 0, 3, 1, 4))
            q, k, v = (qkv[0], qkv[1], qkv[2])
            sm = jnp.exp(jnp.minimum(scale_mul_log, jnp.log(jnp.float32(100.0))))
            qn = q / jnp.maximum(jnp.linalg.norm(q, axis=-1, keepdims=True), 1e-12) * sm
            kn = k / jnp.maximum(jnp.linalg.norm(k, axis=-1, keepdims=True), 1e-12)
            scores = jnp.einsum('bhqd,bhkd->bhqk', qn, kn) + attn_bias
            p = jax.nn.softmax(scores, axis=-1)
            o = jnp.einsum('bhqk,bhkd->bhqd', p, v)
            o = jnp.transpose(o, (0, 2, 1, 3)).reshape(Bs, Lx, Cx)
            return o @ Wproj.T + bproj
        x = x + attn(_ln(x) * (scale1 + 1.0) + shift1) * gamma1
        h = _gelu_tanh((_ln(x) * (scale2 + 1.0) + shift2) @ Wfc1.T + bfc1)
        x = x + (h @ Wfc2.T + bfc2) * gamma2
        return x

    def _L1_cond_ref(x, pos_ids, time_emb, ln1_w, ln1_tw, ln2_w, ln2_tw, Wq, Wk, Wv, Wo, Wg, Wu, Wd):
        import jax, jax.numpy as jnp
        import numpy as np
        HIDDEN, NQ, NKV, HD, INTER = (256, 8, 1, 32, 1024)
        B, S = (4, 256)
        EPS = 1e-06
        ROPE_BASE = 10000.0

        def ada_rms(x, t, w, tw):
            n = x * jax.lax.rsqrt(jnp.mean(jnp.square(x), axis=-1, keepdims=True) + EPS)
            scale = t @ tw.T
            return n * (w * (1.0 + scale))[:, None, :]

        def apply_rope(x, pos_ids):
            half = HD // 2
            inv_freq = 1.0 / ROPE_BASE ** (jnp.arange(0, HD, 2, dtype=jnp.float32) / HD)
            ang = pos_ids.astype(jnp.float32)[:, :, None] * inv_freq
            cos = jnp.concatenate([jnp.cos(ang), jnp.cos(ang)], axis=-1)[:, None]
            sin = jnp.concatenate([jnp.sin(ang), jnp.sin(ang)], axis=-1)[:, None]
            x1, x2 = (x[..., :half], x[..., half:])
            rot = jnp.concatenate([-x2, x1], axis=-1)
            return x * cos + rot * sin
        b, s, _ = x.shape
        g = NQ // NKV
        res = x
        h = ada_rms(x, time_emb, ln1_w, ln1_tw)
        q = (h @ Wq.T).reshape(b, s, NQ, HD).transpose(0, 2, 1, 3)
        k = (h @ Wk.T).reshape(b, s, NKV, HD).transpose(0, 2, 1, 3)
        v = (h @ Wv.T).reshape(b, s, NKV, HD).transpose(0, 2, 1, 3)
        q = apply_rope(q, pos_ids)
        k = apply_rope(k, pos_ids)
        qg = q.reshape(b, NKV, g, s, HD)
        scores = jnp.einsum('bkgsd,bktd->bkgst', qg, k) / jnp.sqrt(jnp.float32(HD))
        attn = jax.nn.softmax(scores, axis=-1)
        ctx = jnp.einsum('bkgst,bktd->bkgsd', attn, v)
        ctx = ctx.reshape(b, NQ, s, HD).transpose(0, 2, 1, 3).reshape(b, s, NQ * HD)
        x = res + ctx @ Wo.T
        res = x
        h = ada_rms(x, time_emb, ln2_w, ln2_tw)
        mlp = jax.nn.silu(h @ Wg.T) * (h @ Wu.T) @ Wd.T
        return res + mlp
    x = _L0_cond_ref(x, cond_2048, mask_1x1xSxS_ff0, L0_cond_Wqkv, L0_cond_q_bias, L0_cond_v_bias, L0_cond_scale_mul_log, L0_cond_Wproj, L0_cond_bproj, L0_cond_Wada, L0_cond_bada, L0_cond_Wfc1, L0_cond_bfc1, L0_cond_Wfc2, L0_cond_bfc2)
    x = _L1_cond_ref(x, pos_BxS, cond_2048, L1_cond_ln1_w, L1_cond_ln1_tw, L1_cond_ln2_w, L1_cond_ln2_tw, L1_cond_Wq, L1_cond_Wk, L1_cond_Wv, L1_cond_Wo, L1_cond_Wg, L1_cond_Wu, L1_cond_Wd)
    return x

_drawn_inputs = setup_inputs


def setup_inputs(seed=0):
    import zlib

    import numpy as np

    out = dict(_drawn_inputs(seed))
    spreads = {'L0_cond_q_bias': (0.0, 0.8),
     'L0_cond_v_bias': (0.0, 0.8),
     'L0_cond_scale_mul_log': (1.3862943649291992, 0.6),
     'L0_cond_bproj': (0.0, 0.369),
     'L0_cond_bada': (0.0, 0.414),
     'L0_cond_bfc1': (0.0, 0.8),
     'L0_cond_bfc2': (0.0, 0.374),
     'L1_cond_ln1_w': (1.0, 0.6),
     'L1_cond_ln2_w': (1.0, 0.6)}
    factors = {'L0_cond_Wqkv': 8.0,
     'L0_cond_Wproj': 6.089,
     'L1_cond_ln1_tw': 8.0,
     'L1_cond_ln2_tw': 16.369,
     'L1_cond_Wq': 8.0,
     'L1_cond_Wk': 8.0,
     'L1_cond_Wv': 5.177,
     'L1_cond_Wo': 5.208,
     'L1_cond_Wg': 4.241,
     'L1_cond_Wu': 4.115,
     'L1_cond_Wd': 4.006}
    for name, (base, spread) in spreads.items():
        noise = np.random.default_rng([zlib.crc32(name.encode()), seed]).standard_normal(out[name].shape)
        drawn = base * np.exp(spread * noise) if base else spread * noise
        out[name] = jnp.asarray(drawn.astype(out[name].dtype))
    for name, factor in factors.items():
        out[name] = (out[name] * factor).astype(out[name].dtype)
    return out
```

```python
from contextlib import ExitStack

import numpy as np

import concourse.bass as bass
from concourse import mybir

F32 = mybir.dt.float32
F32R = mybir.dt.float32r
F16 = mybir.dt.float16
I32 = mybir.dt.int32
ALU = mybir.AluOpType
ACT = mybir.ActivationFunctionType
AX_X = mybir.AxisListType.X

P = 128
N_SEQ, C, HID = 8, 256, 1024
PAIRS = N_SEQ // 2
CT = C // P
FT = HID // P
H0, D0 = 16, 16
H1, D1 = 8, 32
QUAD = 32
QKV1 = C + 2 * D1
LN_EPS = 1e-6
NORM_FLOOR = 1e-24
MAX_LOG_SCALE = float(np.log(np.float32(100.0)))
GELU_C = float(np.sqrt(2.0 / np.pi).astype(np.float32))
SCORE_SCALE1 = float(1.0 / np.sqrt(np.float32(D1)))
ROUND_MAGIC = 1.5 * 2.0 ** 23
TWO_PI = 2.0 * np.pi
PI_1 = 6.28125
PI_2 = float(np.float32(np.floor((TWO_PI - PI_1) * 2 ** 21) / 2 ** 21))
PI_3 = float(np.float32(TWO_PI - PI_1 - PI_2))
SIN_LIMIT = 3.1415925

ROUNDS = [(0, 0), (1, 0), (0, 1), (1, 1), (2, 0), (3, 0), (2, 1), (3, 1)]
ROUND_OF = {pl: r for r, pl in enumerate(ROUNDS)}
STAGE = 5

ADA = {"gamma1": 0, "gamma2": 1, "scale1": 2, "scale2": 3, "shift1": 4, "shift2": 5}
WIDE = ("Wfc2", "Wd")
CHUNKS = ([("ada", ADA["scale1"]), ("ada", ADA["shift1"])]
          + [("Wqkv", 2 * i) for i in range(3)]
          + [("ada", ADA["gamma1"]), ("ada", ADA["gamma2"]), ("Wproj", 0),
             ("ada", ADA["scale2"]), ("ada", ADA["shift2"]), ("tw1", 0), ("tw2", 0)]
          + [("Wfc1", 2 * i) for i in range(4)]
          + [("Wfc2", i) for i in range(4)]
          + [("Wq", 0), ("Wkv", 0), ("Wo", 0)]
          + [(w, 2 * i) for i in range(4) for w in ("Wg", "Wu")]
          + [("Wd", i) for i in range(4)])
N_CHUNKS = len(CHUNKS)
CHUNK_AT = {c: i for i, c in enumerate(CHUNKS)}
IS_ADA = {i: n for n, i in enumerate(i for i, c in enumerate(CHUNKS) if c[0] in ("ada", "tw1", "tw2"))}
LAST_CHUNK = {}
for _i, _c in enumerate(CHUNKS):
    LAST_CHUNK[_c[0]] = _i
MOD_OF = {("ada", 2): 0, ("ada", 4): 1, ("ada", 3): 2, ("ada", 5): 3, ("tw1", 0): 4, ("tw2", 0): 5}


def attention_steps(r):
    pair, layer = ROUNDS[r]
    n0, n1 = 2 * r, 2 * r + 1
    s = []
    for n in (n0, n1):
        s += [("norm_stats", "a", n, 0.5)]
    s += [("wait", 2.0)]
    for n in (n0, n1):
        s += [("norm_apply", "a", n, 0.0), ("norm_mod", "a", n, 2.0)]
    if layer == 0:
        for n in (n0, n1):
            s += [("qk_product", n, 1.0), ("v_product", n, 1.0)]
        s += [("wait", 2.0)]
        for n in (n0, n1):
            s += [("qk_scale", n, 1.2)]
        s += [("qk_turn", n0, 1.5), ("qk_turn", n1, 0.5)]
    else:
        for n in (n0, n1):
            s += [("qkv1_product", n, 1.0), ("rope", n, 1.0)]
        for n in (n0, n1):
            s += [("qk1_turn", n, 0.7)]
    groups = [4 * n0 + i for i in range(8)]
    step = 2.2 if layer == 0 else 1.3
    for t in range(len(groups) + 2):
        if t < len(groups):
            s += [("scores", groups[t], 0.0), ("softmax", groups[t], step / 2)]
        if 0 <= t - 1 < len(groups):
            s += [("turn_probs", groups[t - 1], step / 4)]
        if 0 <= t - 2 < len(groups):
            g = groups[t - 2]
            s += [("values", g, step / 4)]
            if g % 4 == 3:
                s += [("attn_out", g // 4, 0.3)]
        if t - 2 == 5:
            s += [("project", n0, 0.3)]
    s += [("wait", 1.0), ("project", n1, 1.0)]
    return s


def mlp_steps(r):
    pair, layer = ROUNDS[r]
    n0, n1 = 2 * r, 2 * r + 1
    s = []
    for n in (n0, n1):
        s += [("norm_stats", "m", n, 0.5)]
    s += [("wait", 2.0)]
    for n in (n0, n1):
        s += [("norm_apply", "m", n, 0.0), ("norm_mod", "m", n, 2.0)]
    s += [("wait", 1.0)]
    if layer == 0:
        for c in range(FT // 2):
            s += [("fc1", r, c, 0.0)]
            s += [("gelu", r, c, 3.0)]
    else:
        for f in range(FT):
            s += [("gate_up", r, f, 2.0)]
    s += [("wait", 1.0)]
    s += [("down", n0, 3.0), ("down", n1, 3.0)]
    return s


def make_schedule(tune=None):
    tune = tune or {}
    slot = tune.get("slot", 32.0)
    start = tune.get("start", 14.0)
    timed = []

    def place(steps, at, span):
        total = sum(x[-1] for x in steps)
        for x in steps:
            if x[0] != "wait":
                timed.append((at, len(timed), x[:-1]))
            at += x[-1] * span / total

    for r in range(len(ROUNDS)):
        place(attention_steps(r), start + slot * r, slot)
        place(mlp_steps(r), start + slot * (r + 1), slot)
    timed.append((-1.0, -1, ("conditioning",)))
    timed.append((1.0, len(timed), ("rope_tables",)))
    at = 0.0
    pace = tune.get("pace", 1.3)
    for c in range(N_CHUNKS):
        timed.append((at, len(timed), ("prepare", c)))
        if c in IS_ADA:
            timed.append((at + 1.5 * pace, len(timed), ("modulation", c)))
        at += pace if c < 8 else tune.get("pace2", 2.0)
        if c == CHUNK_AT[("ada", ADA["gamma2"])]:
            timed.append((at + 1.5 * pace, len(timed), ("gamma_store",)))
            for p in (0, 1):
                timed.append((at + 1.5 * pace + 0.1, len(timed), ("gamma_load", p)))
    for p in (2, 3):
        timed.append((start + slot * (ROUND_OF[(p, 0)]) + 5.0, len(timed), ("gamma_load", p)))
    return [x for _, _, x in sorted(timed, key=lambda v: (v[0], v[1]))]


SCHEDULE = make_schedule()

BANKS = ["turn", "linear", "hidden0", "hidden1", "scores0", "scores1", "probs", "output"]


def bank_plan():
    used = {b: 0 for b in BANKS}
    flip = {"hidden": 0, "scores": 0}
    plan = {}

    def use(key, kind):
        b = kind
        if kind in flip:
            b = f"{kind}{flip[kind] % 2}"
            flip[kind] += 1
        plan[key] = (b, used[b])
        used[b] += 1

    for step in SCHEDULE:
        k = step[0]
        if k in ("conditioning", "modulation", "norm_apply", "qk1_turn"):
            use(step, "turn")
        elif k == "qk_turn":
            use(("q_turn", step[1]), "turn")
            use(("k_turn", step[1]), "turn")
        elif k in ("qk_product", "v_product", "qkv1_product", "project", "down"):
            use(step, "linear")
        elif k in ("prepare", "fc1", "gate_up"):
            use(step, "hidden")
        elif k == "scores":
            use(step, "scores")
        elif k == "turn_probs":
            use(step, "probs")
        elif k == "values" and step[1] % 4 == 0:
            use(("output", step[1] // 4), "output")
    return plan


PLAN = bank_plan()


def seq_of(n):
    return 2 * ROUNDS[n // 2][0] + n % 2


def layer_of(n):
    return ROUNDS[n // 2][1]


def heads_of(group):
    i = group % 4
    tiles = H0 // 4 if layer_of(group // 4) == 0 else H1 // 4
    return [4 * g + i for g in range(tiles)]


def build(nc, x, cond, pos, mask, w, out):
    with ExitStack() as ctx:
        def sb(name, shape, dt=F32):
            return ctx.enter_context(nc.sbuf_tensor(name, shape, dt))

        def sem(name):
            return ctx.enter_context(nc.semaphore(name))

        psum = {b: ctx.enter_context(nc.psum_tensor("ps_" + b, [P, 512], F32)) for b in BANKS}
        filled = {b: sem("filled_" + b) for b in BANKS}
        freed = {b: sem("freed_" + b) for b in BANKS}

        def pair_of(name, shape):
            return sb(name + "_hi", shape, F32R), sb(name + "_lo", shape, F32R)

        WT = {"Wqkv": pair_of("WqkvT", [P, CT, 3 * C]), "Wfc1": pair_of("Wfc1T", [P, CT, HID]),
              "Wqkv1": pair_of("Wqkv1T", [P, CT, QKV1]),
              "Wg": pair_of("WgT", [P, CT, HID]), "Wu": pair_of("WuT", [P, CT, HID])}
        WT1 = {"Wproj": sb("WprojT", [P, CT, C]), "Wo": sb("WoT", [P, CT, C]),
               "Wfc2": sb("Wfc2T", [P, FT, C]), "Wd": sb("WdT", [P, FT, C])}
        stage = sb("stage", [P, STAGE, 4 * P])
        ident = sb("ident", [P, P])
        ident16 = sb("ident16", [P, P], F16)
        ones_half = sb("ones_half", [P, 2, QUAD])
        ones_quad = sb("ones_quad", [P, QUAD])
        minus_half = sb("minus_half", [P, 2 * H0])
        inv_freq = sb("inv_freq", [P, D1 // 2])

        g_u = sb("g_u", [P, 2, 2 * 2 * P])
        g_b = sb("g_b", [P, 2, 2 * 2 * P])
        g_h = sb("g_h", [P, FT, 2 * P])
        adaT = g_b[:, :, :].rearrange("p s (a b) -> p s a b", a=CT)
        cond8, cond_t, silu8 = [g_h[0:N_SEQ, i, :] for i in range(3)]
        bada8 = g_h[0:N_SEQ, 3:5, :].rearrange("p a b -> p (a b)")
        gamma8 = g_h[0:N_SEQ, 5:7, :].rearrange("p a b -> p (a b)")
        vec_rows = g_h[0:12 + FT + 2 * CT, 7, 0:P]
        red = g_u[:, :, :].rearrange("p a b -> p (a b)")[:, 0:3 * 2 * N_SEQ * D1 // 2].rearrange(
            "p (a b c d) -> p a b c d", a=3, b=2, c=N_SEQ)
        ang = g_u[:, :, :].rearrange("p a b -> p (a b)")[:, 3 * 2 * N_SEQ * D1 // 2:7 * N_SEQ * D1 // 2].rearrange(
            "p (c d) -> p c d", c=N_SEQ)

        N_VEC = 12 + FT + 2 * CT
        cols = sb("cols", [P, 4 * N_SEQ + N_VEC])
        V0 = 4 * N_SEQ
        V_BADA, V_BFC1, V_LN1, V_LN2 = V0, V0 + 12, V0 + 12 + FT, V0 + 12 + FT + CT
        modul = sb("modul", [P, 6, CT, N_SEQ])
        gamma_dram = nc.dram_tensor("gamma_scratch", (N_SEQ, 2 * C), F32).ap()
        gamma = sb("gamma", [P, 2, 2, 2 * C])
        qk_bias = sb("qk_bias", [P, 2 * C])
        v_bias = sb("v_bias", [P, C])
        res_bias = sb("res_bias", [P, 2, C])
        head_scale = sb("head_scale", [P, H0])
        head_log = sb("head_log", [P, H0])
        bias_mask = sb("bias_mask", [P, P])
        pos_i = sb("pos_i", [P, N_SEQ], I32)
        pos_f = sb("pos_f", [P, N_SEQ])
        HALF = D1 // 2
        turns = sb("turns", [P, 2, N_SEQ, HALF])
        cos_t = sb("cos_t", [P, N_SEQ, HALF])
        sin_t = sb("sin_t", [P, N_SEQ, 2, HALF])

        X = sb("X", [P, N_SEQ, C])
        stats = sb("stats", [P, 32, 6])
        mean_var = sb("mean_var", [P, 32, 2])
        msq = sb("msq", [P, 32, 2])
        rstd = sb("rstd", [P, 32, 1])
        NM = {"a": 0, "m": 1}
        xn = sb("xn", [P, 2, 2, C])
        h_full = xn[:, :, :, :].rearrange("p m j (c t) -> p m j c t", t=P)
        h_hi = sb("h_hi", [P, 2, CT, 2 * P], F32R)
        h_lo = sb("h_lo", [P, 2, CT, 2 * P], F32R)
        qk = sb("qk", [P, 2, 2 * C])
        qk_ss = sb("qk_ss", [P, 2, 2 * H0])
        qk_fl = sb("qk_fl", [P, 2, 2 * H0])
        qk_r = sb("qk_r", [P, 2, 2 * H0])
        qk_rs = sb("qk_rs", [P, 2, 2 * H0])
        qk_n = sb("qk_n", [P, 2, 2 * C])
        qk_sq = qk_n
        qk_pack = sb("qk_pack", [P, 2, 3, H0, QUAD], F16)
        qkT = sb("qkT", [P, 2, 3, 4, P], F16)
        v_pad = sb("v_pad", [P, 2, H0, QUAD])
        qkv1 = sb("qkv1", [P, 2, QKV1])
        rope_c = sb("rope_c", [P, 9, 2, HALF])
        rope_s = sb("rope_s", [P, 9, 2, HALF])
        qk1_rot = sb("qk1_rot", [P, 2, 12, D1])
        qk1T = sb("qk1T", [P, 2, 3, P])
        z = sb("z", [P, 2, 4, P])
        neg_max = sb("neg_max", [P, 2, 4])
        neg_max_s = sb("neg_max_s", [P, 2, 4])
        probs = z
        probsT = sb("probsT", [P, 2, 4, P])
        rden = sb("rden", [P, CT, P])
        o_full = sb("o_full", [P, 2, CT, P])
        res_t = sb("res_t", [P, 2, 2, C])
        g_a = sb("g_a", [P, 2, 2 * 2 * P])

        stage_loaded = [sem(f"stage_loaded{i}") for i in range(STAGE)]
        small_loaded = sem("small_loaded")
        vec_loaded = sem("vec_loaded")
        x_loaded = [sem(f"x_loaded{i}") for i in range(PAIRS)]
        gamma_stored, out_stored = sem("gamma_stored"), sem("out_stored")
        gamma_loaded = [sem(f"gamma_loaded{i}") for i in range(PAIRS)]
        consts_set = sem("consts_set")
        zeroed, half_done = sem("zeroed"), sem("half_done")
        cond_tanh, cond_silu, cols_ready = sem("cond_tanh"), sem("cond_silu"), sem("cols_ready")
        silu_mid = sem("silu_mid")
        weights_turned = sem("weights_turned")
        weight_hi, weight_ready = sem("weight_hi"), sem("weight_ready")
        ada_used, mod_ready, gamma_ready = sem("ada_used"), sem("mod_ready"), sem("gamma_ready")
        table_step, angles_ready, table_ready = sem("table_step"), sem("angles_ready"), sem("table_ready")
        scale_clipped, scale_ready = sem("scale_clipped"), sem("scale_ready")
        stats_mid, stats_ready = [{k: sem(f"{s}_{k}") for k in "am"} for s in ("stats_mid", "stats_ready")]
        stats_ms = {k: sem(f"stats_ms_{k}") for k in "am"}
        rstd_mid, rstd_ready = [{k: sem(f"{s}_{k}") for k in "am"} for s in ("rstd_mid", "rstd_ready")]
        xn_ready, h_ready = [{k: sem(f"{s}_{k}") for k in "am"} for s in ("xn_ready", "h_ready")]
        h_hi_ready, h_lo_ready = [{k: sem(f"{s}_{k}") for k in "am"} for s in ("h_hi_ready", "h_lo_ready")]
        h_used = {k: sem(f"h_used_{k}") for k in "am"}
        qk_ready, qk_squared, qk_summed = sem("qk_ready"), sem("qk_squared"), sem("qk_summed")
        qk_floor, qk_root, qk_rnorm = sem("qk_floor"), sem("qk_root"), sem("qk_rnorm")
        qk_normed, qk_hi_ready, qk_packed = sem("qk_normed"), sem("qk_hi_ready"), sem("qk_packed")
        qk_lo_ready, v_ready, qkT_ready = sem("qk_lo_ready"), sem("v_ready"), sem("qkT_ready")
        qk_turned = sem("qk_turned")
        qkv1_ready, rope_cos, rope_sin, rope_ready = (sem("qkv1_ready"), sem("rope_cos"), sem("rope_sin"),
                                                      sem("rope_ready"))
        z_ready, max_ready, max_mid, exp_ready = sem("z_ready"), sem("max_ready"), sem("max_mid"), sem("exp_ready")
        values_summed = sem("values_summed")
        rden_ready, o_ready, o_hi_ready, o_lo_ready = (sem("rden_ready"), sem("o_ready"), sem("o_hi_ready"),
                                                       sem("o_lo_ready"))
        o_used = sem("o_used")
        res_mid = {k: sem(f"res_mid_{k}") for k in "am"}
        res_scaled = {k: sem(f"res_scaled_{k}") for k in "am"}
        res_ready = {k: sem(f"res_ready_{k}") for k in "am"}
        g_u_ready, g_sq, g_poly, g_inner, g_tanh, g_full, g_hi_ready, g_lo_ready = [
            sem(s) for s in ("g_u_ready", "g_sq", "g_poly", "g_inner", "g_tanh", "g_full", "g_hi_ready",
                             "g_lo_ready")]
        g_used, g_gated = sem("g_used"), sem("g_gated")

        def mlp_ord(r, c):
            return sum((FT // 2 if ROUNDS[q][1] == 0 else FT) for q in range(r)) + c

        def ord0(n):
            return 2 * sum(1 for q in range(n // 2) if ROUNDS[q][1] == 0) + n % 2

        def ord1(n):
            return 2 * sum(1 for q in range(n // 2) if ROUNDS[q][1] == 1) + n % 2

        def splits_before(c):
            return sum(1 for q in range(c) if q not in IS_ADA and CHUNKS[q][0] not in WT1)

        def gu_ord(r, f):
            return sum(1 for q in range(r) if ROUNDS[q][1] == 1) * FT + f

        def of_ord1(o):
            return [n for n in range(2 * len(ROUNDS)) if layer_of(n) == 1][o]

        def fc_ord(r, c):
            return sum(1 for q in range(r) if ROUNDS[q][1] == 0) * (FT // 2) + c

        def ready_before(kind, n):
            pair, layer = ROUNDS[n // 2]
            if kind == "m":
                return res_ready["a"], n + 1
            if layer == 0:
                return x_loaded[pair], 16
            return res_ready["m"], 2 * ROUND_OF[(pair, 0)] + n % 2 + 1

        def weight_views(c, bank):
            name, i = CHUNKS[c]
            src = bank[:, :].rearrange("p (a b) -> p a b", b=256)
            if name in WIDE:
                hi, lo = WT1[name], WT1[name]
                r, c0 = i // 2, 4 * (i % 2)
                sl = (slice(None), slice(c0, c0 + 4), slice(r * P, (r + 1) * P))
                return hi[sl], lo[sl], bank[:, :].rearrange("p (a b) -> p a b", b=P)
            if name == "Wkv":
                hi, lo = WT["Wqkv1"]
                sl = (slice(None), slice(None), slice(C, QKV1))
                return hi[sl], lo[sl], bank[:, 0:4 * D1].rearrange("p (a b) -> p a b", b=2 * D1)
            if name == "Wq":
                hi, lo = WT["Wqkv1"]
                sl = (slice(None), slice(None), slice(0, C))
                return hi[sl], lo[sl], src
            hi, lo = WT[name] if name in WT else (WT1[name], WT1[name])
            sl = (slice(None), slice(None), slice(i * P, (i + 2) * P))
            return hi[sl], lo[sl], src

        N_SMALL = 9
        block = ctx.enter_context(nc.Block())

        @block.sync
        def _(sp):
            def bcast(v, rows):
                return v.partition_broadcast(rows)

            sp.dma_start(cond8[:, :], cond).then_inc(vec_loaded, 16)
            sp.dma_start(vec_rows[0:12, :], w["bada"].rearrange("(r p) -> r p", p=P)).then_inc(vec_loaded, 16)
            sp.dma_start(vec_rows[12:12 + FT, :], w["bfc1"].rearrange("(r p) -> r p", p=P)).then_inc(vec_loaded, 16)
            sp.dma_start(vec_rows[20:22, :], w["ln1_w"].rearrange("(r p) -> r p", p=P)).then_inc(vec_loaded, 16)
            sp.dma_start(vec_rows[22:24, :], w["ln2_w"].rearrange("(r p) -> r p", p=P)).then_inc(vec_loaded, 16)

            def load_chunk(c):
                name, i = CHUNKS[c]
                if c >= STAGE:
                    sp.wait_ge(weights_turned, c - STAGE + 1)
                dst = stage[:, c % STAGE, :]
                if name == "Wkv":
                    d2 = dst[:, 0:C]
                    sp.dma_start(d2[0:D1, :], w["Wk"]).then_inc(stage_loaded[c % STAGE], 16)
                    sp.dma_start(d2[D1:2 * D1, :], w["Wv"]).then_inc(stage_loaded[c % STAGE], 16)
                    return
                if name == "ada":
                    src = w["Wada"][i * C:(i + 1) * C, :].rearrange("(t p) i -> p t i", p=P)
                elif name in WIDE:
                    src = w[name][(i // 2) * P:(i // 2 + 1) * P, (i % 2) * 512:(i % 2 + 1) * 512]
                    sp.dma_start(dst, src).then_inc(stage_loaded[c % STAGE], 16)
                    return
                else:
                    src = w[name][i * P:(i + 2) * P, :].rearrange("(t p) i -> p t i", p=P)
                sp.dma_start(dst.rearrange("p (t i) -> p t i", t=2), src).then_inc(stage_loaded[c % STAGE], 16)

            def load_x(p):
                sp.dma_start(X[:, 2 * p:2 * p + 2, :],
                             x[2 * p:2 * p + 2].rearrange("n t c -> t n c")).then_inc(x_loaded[p], 16)

            load_chunk(0)
            load_x(0)
            load_chunk(1)
            for dst, src in ((pos_i[:, :], pos), (head_log[:, :], bcast(w["sml"], P)),
                             (qk_bias[:, 0:C], bcast(w["q_bias"], P)), (v_bias[:, :], bcast(w["v_bias"], P)),
                             (res_bias[:, 0, :], bcast(w["bproj"], P)), (res_bias[:, 1, :], bcast(w["bfc2"], P)),
                             (bias_mask[:, :], mask), (bada8[:, 0:C], bcast(w["bada"][0:C], N_SEQ)),
                             (bada8[:, C:2 * C], bcast(w["bada"][C:2 * C], N_SEQ))):
                sp.dma_start(dst, src).then_inc(small_loaded, 16)
            for c in range(2, STAGE):
                load_chunk(c)
            load_x(1)
            for step in SCHEDULE:
                if step[0] == "prepare":
                    c = step[1]
                    if c + STAGE < N_CHUNKS:
                        load_chunk(c + STAGE)
                    if c == 12:
                        load_x(2)
                        load_x(3)
                elif step[0] == "gamma_store":
                    sp.wait_ge(gamma_ready, 2)
                    sp.dma_start(gamma_dram, gamma8[:, :]).then_inc(gamma_stored, 16)
                    sp.wait_ge(gamma_stored, 16)
                elif step[0] == "gamma_load":
                    p = step[1]
                    if p >= 2:
                        sp.wait_ge(res_scaled["m"], 2 * sum(1 for q in range(ROUND_OF[(p - 2, 0)] + 1)
                                                            if ROUNDS[q][1] == 0))
                    for j in range(2):
                        sp.dma_start(gamma[:, p % 2, j, :],
                                     gamma_dram[2 * p + j].partition_broadcast(P)).then_inc(gamma_loaded[p], 16)
                elif step[0] == "down" and layer_of(step[1]) == 1:
                    n = step[1]
                    sp.wait_ge(res_ready["m"], n + 1)
                    sp.dma_start(out[seq_of(n)], X[:, seq_of(n), :]).then_inc(out_stored, 16)
            sp.wait_ge(out_stored, 16 * N_SEQ)

        @block.gpsimd
        def _(pool):
            pool.memset(ident[:, :], 0.0).then_inc(zeroed, 1)
            pool.wait_ge(zeroed, 1)
            pool.affine_select(out=ident[:, :], in_=ident[:, :], compare_op=ALU.not_equal, fill=1.0, base=0,
                               pattern=[[-1, P]], channel_multiplier=1).then_inc(consts_set, 1)
            pool.memset(minus_half[:, :], -0.5)
            pool.memset(ones_half[:, :, :], 0.0).then_inc(zeroed, 1)
            pool.wait_ge(zeroed, 2)
            pool.memset(ones_half[:, 0, 0:D0], 1.0)
            pool.memset(ones_half[:, 1, D0:2 * D0], 1.0)
            pool.memset(ones_quad[:, :], 1.0)
            pool.memset(v_pad[:, :, :, :], 0.0)
            pool.memset(qk_bias[:, C:2 * C], 0.0)
            for f in range(HALF):
                pool.memset(inv_freq[:, f:f + 1], float(np.float32(1.0) / np.float32(
                    np.float32(10000.0) ** np.float32(2.0 * f / D1))))
            pool.wait_ge(consts_set, 1)
            pool.tensor_copy(ident16[:, :], ident[:, :]).then_inc(consts_set, 1)

            def norm_stats(kind, n):
                k = NM[kind] * 16 + n
                pool.wait_ge(stats_ready[kind], n + 1)
                pool.tensor_scalar(msq[:, k, 1:2], msq[:, k, 0:1], LN_EPS, None, ALU.add).then_inc(rstd_mid[kind], 1)
                pool.wait_ge(rstd_mid[kind], n + 1)
                pool.tensor_tensor(rstd[:, k, :], msq[:, k, 1:2], minus_half[:, 0:1],
                                   ALU.pow).then_inc(rstd_ready[kind], 1)

            def norm_mod(kind, n):
                m, j = NM[kind], n % 2
                pool.wait_ge(h_hi_ready[kind], n + 1)
                pool.tensor_tensor(h_lo[:, m, :, j * P:(j + 1) * P], h_full[:, m, j, :, :],
                                   h_hi[:, m, :, j * P:(j + 1) * P].bitcast(F32),
                                   ALU.subtract).then_inc(h_lo_ready[kind], 1)

            def qk_product(n):
                o, j = ord0(n), n % 2
                pool.wait_ge(qk_floor, o + 1)
                pool.tensor_tensor(qk_r[:, j, :], qk_fl[:, j, :], minus_half[:, :], ALU.pow).then_inc(qk_root, 1)
                pool.wait_ge(qk_root, o + 1)
                if o == 0:
                    pool.wait_ge(scale_ready, 1)
                if o >= 2:
                    pool.wait_ge(qk_normed, o - 1)
                pool.tensor_tensor(qk_rs[:, j, 0:H0], qk_r[:, j, 0:H0], head_scale[:, :], ALU.mult)
                pool.tensor_copy(qk_rs[:, j, H0:2 * H0], qk_r[:, j, H0:2 * H0]).then_inc(qk_rnorm, 1)

            def qk_scale(n):
                o, j = ord0(n), n % 2
                pool.wait_ge(qk_lo_ready, o + 1)
                pool.tensor_copy(qk_pack[:, j, 2, :, 0:D0], qk_pack[:, j, 0, :, D0:2 * D0])
                pool.tensor_copy(qk_pack[:, j, 2, :, D0:2 * D0], qk_pack[:, j, 0, :, 0:D0]).then_inc(qk_packed, 1)

            def residual(kind, n):
                if layer_of(n) == 0:
                    pool.wait_ge(res_scaled[kind], ord0(n) + 1)
                    s = seq_of(n)
                    pool.tensor_tensor(X[:, s, :], X[:, s, :], res_t[:, NM[kind], 1, :],
                                       ALU.add).then_inc(res_ready[kind], 1)

            def gelu(r, c):
                o = fc_ord(r, c)
                pool.wait_ge(g_sq, o + 1)
                if o >= 2:
                    pool.wait_ge(g_inner, o - 1)
                else:
                    pool.wait_ge(ada_used, len(IS_ADA))
                pool.tensor_scalar(g_b[:, o % 2, :], g_a[:, o % 2, :], 0.044715, 1.0, ALU.mult,
                                   ALU.add).then_inc(g_poly, 1)

            for step in SCHEDULE:
                k, a = step[0], step[1:]
                if k == "norm_stats":
                    norm_stats(*a)
                elif k == "norm_mod":
                    norm_mod(*a)
                elif k == "qk_product":
                    qk_product(*a)
                elif k == "qk_scale":
                    qk_scale(*a)
                elif k == "project":
                    residual("a", *a)
                elif k == "down":
                    residual("m", *a)
                elif k == "gelu":
                    gelu(*a)

        @block.scalar
        def _(act):
            def conditioning():
                act.wait_ge(vec_loaded, 16 * 5)
                act.activation(cond_t[:, :], cond8[:, :], ACT.Tanh, scale=0.5).then_inc(cond_tanh, 1)

            def rope_tables():
                act.wait_ge(angles_ready, 1)
                act.activation(sin_t[:, :, 0, :], red[:, 2, 1, :, :], ACT.Sin, scale=-1.0)
                act.activation(sin_t[:, :, 1, :], red[:, 2, 1, :, :], ACT.Sin)
                act.activation(cos_t[:, :, :], red[:, 2, 0, :, :], ACT.Sin).then_inc(table_ready, 1)
                act.wait_ge(scale_clipped, 1)
                act.activation(head_scale[:, :], head_log[:, :], ACT.Exp).then_inc(scale_ready, 1)

            def prepare(c):
                b, t = PLAN[("prepare", c)]
                if c in IS_ADA or CHUNKS[c][0] in WT1:
                    return
                act.wait_ge(filled[b], t + 1)
                hi, _, src = weight_views(c, psum[b])
                act.activation(hi, src, ACT.Copy).then_inc(weight_hi, 1)

            def norm_mod(kind, n):
                m, j = NM[kind], n % 2
                act.wait_ge(h_ready[kind], n + 1)
                if n >= 2:
                    act.wait_ge(h_used[kind], n // 2)
                act.activation(h_hi[:, m, :, j * P:(j + 1) * P], h_full[:, m, j, :, :],
                               ACT.Copy).then_inc(h_hi_ready[kind], 1)

            def qk_product(n):
                o, j = ord0(n), n % 2
                act.wait_ge(qk_ready, o + 1)
                if o >= 2:
                    act.wait_ge(qk_summed, o - 1)
                act.activation(qk_sq[:, j, :], qk[:, j, :], ACT.Square).then_inc(qk_squared, 1)

            def qk_scale(n):
                o, j = ord0(n), n % 2
                act.wait_ge(qk_normed, o + 1)
                if o >= 2:
                    act.wait_ge(qk_turned, o - 1)
                act.activation(qk_pack[:, j, 0:2, :, 0:D0],
                               qk_n[:, j, :].rearrange("p (s h d) -> p s h d", s=2, d=D0),
                               ACT.Copy).then_inc(qk_hi_ready, 1)

            def qkv1_product(n):
                o, j = ord1(n), n % 2
                b, t = PLAN[("qkv1_product", n)]
                act.wait_ge(filled[b], t + 1)
                if o >= 2:
                    act.wait_ge(rope_ready, o - 1)
                if n >= 2:
                    act.wait_ge(values_summed, 4 * (n - 1))
                act.activation(qkv1[:, j, :], psum[b][:, 0:QKV1], ACT.Copy).then_inc(freed[b], 1)

            def softmax(G):
                n = G // 4
                act.wait_ge(max_ready, G + 1)
                if G >= 2:
                    act.wait_ge(filled["probs"], G - 1)
                heads = heads_of(G)
                b, _ = PLAN[("scores", G)]
                for u in range(len(heads)):
                    if layer_of(n) == 0:
                        ins = act.activation(probs[:, G % 2, u, :], z[:, G % 2, u, :], ACT.Exp,
                                             bias=neg_max[:, G % 2, u:u + 1])
                    else:
                        ins = act.activation(probs[:, G % 2, u, :], psum[b][:, u * P:(u + 1) * P], ACT.Exp,
                                             bias=neg_max_s[:, G % 2, u:u + 1], scale=SCORE_SCALE1)
                ins.then_inc(exp_ready, 1)

            def turn_probs(G):
                if G % 2 == 0:
                    return
                b, t = PLAN[("turn_probs", G)]
                U = len(heads_of(G))
                act.wait_ge(filled[b], t + 1)
                if G >= 2:
                    act.wait_ge(values_summed, G - 1)
                act.activation(probsT[:, G % 2, 0:U, :], psum[b][:, 0:U * P].rearrange("p (u q) -> p u q", u=U),
                               ACT.Copy).then_inc(freed[b], 1)

            def gelu(r, c):
                o = fc_ord(r, c)
                b, t = PLAN[("fc1", r, c)]
                act.wait_ge(filled[b], t + 1)
                if o >= 2:
                    act.wait_ge(g_full, mlp_ord(r, c) - 1 if c >= 2 else mlp_ord(r, 0) - (2 - c) + 1)
                for s in range(2):
                    f = 2 * c + s
                    ins = act.activation(g_u[:, o % 2, s * 256:(s + 1) * 256], psum[b][:, s * 256:(s + 1) * 256],
                                         ACT.Identity, bias=cols[:, V_BFC1 + f:V_BFC1 + f + 1])
                ins.then_inc(freed[b], 1)
                act.wait_ge(freed[b], t + 1)
                if o >= 2:
                    act.wait_ge(g_poly, o - 1)
                act.activation(g_a[:, o % 2, :], g_u[:, o % 2, :], ACT.Square).then_inc(g_sq, 1)
                act.wait_ge(g_inner, o + 1)
                act.activation(g_a[:, o % 2, :], g_a[:, o % 2, :], ACT.Tanh, scale=GELU_C).then_inc(g_tanh, 1)

            def gate_up(r, f):
                m = mlp_ord(r, f)
                b, t = PLAN[("gate_up", r, f)]
                act.wait_ge(filled[b], t + 1)
                if m >= 2:
                    act.wait_ge(g_full, m - 1)
                act.activation(g_a[:, f % 2, 0:256], psum[b][:, 0:256], ACT.Tanh, scale=0.5).then_inc(g_tanh, 1)

            for step in SCHEDULE:
                k, a = step[0], step[1:]
                if k == "conditioning":
                    conditioning()
                elif k == "rope_tables":
                    rope_tables()
                elif k == "prepare":
                    prepare(*a)
                elif k == "norm_mod":
                    norm_mod(*a)
                elif k == "qk_product":
                    qk_product(*a)
                elif k == "qk_scale":
                    qk_scale(*a)
                elif k == "qkv1_product":
                    qkv1_product(*a)
                elif k == "softmax":
                    softmax(*a)
                elif k == "turn_probs":
                    turn_probs(*a)
                elif k == "gelu":
                    gelu(*a)
                elif k == "gate_up":
                    gate_up(*a)

        @block.vector
        def _(dve):
            def conditioning():
                dve.wait_ge(cond_tanh, 1)
                dve.scalar_tensor_tensor(out=cond_t[:, :], in0=cond_t[:, :], scalar=1.0, in1=cond8[:, :],
                                         op0=ALU.add, op1=ALU.mult).then_inc(silu_mid, 1)
                dve.wait_ge(silu_mid, 1)
                dve.tensor_scalar(silu8[:, :], cond_t[:, :], 0.5, None, ALU.mult).then_inc(cond_silu, 1)
                dve.wait_ge(filled["turn"], 1)
                dve.tensor_copy(cols[:, :], psum["turn"][:, 0:V0 + N_VEC]).then_inc(freed["turn"], 1)

            tick = [0]

            def link(ins):
                ins.then_inc(table_step, 1)
                tick[0] += 1
                dve.wait_ge(table_step, tick[0])

            def rope_tables():
                dve.wait_ge(small_loaded, 16 * N_SMALL)
                dve.tensor_scalar(head_log[:, :], head_log[:, :], MAX_LOG_SCALE, None,
                                  ALU.min).then_inc(scale_clipped, 1)
                dve.wait_ge(consts_set, 2)
                link(dve.tensor_copy(pos_f[:, :], pos_i[:, :]))
                link(dve.tensor_tensor(ang[:, :, :], pos_f[:, :].unsqueeze(2).to_broadcast([P, N_SEQ, HALF]),
                                       inv_freq[:, :].unsqueeze(1).to_broadcast([P, N_SEQ, HALF]), ALU.mult))
                dve.tensor_scalar(red[:, 0, 0, :, :], ang[:, :, :], 1.0 / TWO_PI, 0.25, ALU.mult, ALU.add)
                link(dve.tensor_scalar(red[:, 0, 1, :, :], ang[:, :, :], 1.0 / TWO_PI, None, ALU.mult))
                link(dve.tensor_scalar(turns[:, :, :, :], red[:, 0, :, :, :], ROUND_MAGIC, ROUND_MAGIC, ALU.add,
                                       ALU.subtract))
                a2 = ang[:, :, :].rearrange("p n f -> p (n f)").unsqueeze(1).to_broadcast([P, 2, N_SEQ * HALF])
                fl = [red[:, i, :, :, :].rearrange("p s n f -> p s (n f)") for i in range(3)]
                tf = turns[:, :, :, :].rearrange("p s n f -> p s (n f)")
                link(dve.scalar_tensor_tensor(out=fl[0], in0=tf, scalar=-PI_1, in1=a2, op0=ALU.mult, op1=ALU.add))
                link(dve.scalar_tensor_tensor(out=fl[1], in0=tf, scalar=-PI_2, in1=fl[0], op0=ALU.mult,
                                              op1=ALU.add))
                link(dve.scalar_tensor_tensor(out=fl[0], in0=tf, scalar=-PI_3, in1=fl[1], op0=ALU.mult,
                                              op1=ALU.add))
                dve.tensor_copy(red[:, 1, 1, :, :], red[:, 0, 1, :, :])
                link(dve.tensor_scalar(red[:, 1, 0, :, :], red[:, 0, 0, :, :], float(np.pi / 2), None, ALU.add))
                dve.tensor_scalar(red[:, 2, :, :, :], red[:, 1, :, :, :], SIN_LIMIT, -SIN_LIMIT, ALU.min,
                                  ALU.max).then_inc(angles_ready, 1)

            def prepare(c):
                b, t = PLAN[("prepare", c)]
                if c in IS_ADA:
                    o = IS_ADA[c]
                    dve.wait_ge(filled[b], t + 1)
                    if o >= 2:
                        dve.wait_ge(ada_used, o - 1)
                    dve.tensor_copy(adaT[:, o % 2, :, :], psum[b][:, :].rearrange("p (a b) -> p a b", b=C)
                                    ).then_inc(weight_ready, 1)
                    dve.wait_ge(weight_ready, c + 1)
                    dve.sem_inc(freed[b], 1)
                    return
                hi, lo, src = weight_views(c, psum[b])
                if CHUNKS[c][0] in WT1:
                    dve.wait_ge(filled[b], t + 1)
                    dve.tensor_scalar(hi, src, 0.5 if CHUNKS[c][0] == "Wfc2" else 1.0, None,
                                      ALU.mult).then_inc(weight_ready, 1)
                else:
                    dve.wait_ge(weight_hi, splits_before(c) + 1)
                    dve.tensor_tensor(lo, src, hi.bitcast(F32), ALU.subtract).then_inc(weight_ready, 1)
                dve.wait_ge(weight_ready, c + 1)
                dve.sem_inc(freed[b], 1)

            def modulation(c):
                b, t = PLAN[("modulation", c)]
                dve.wait_ge(filled[b], t + 1)
                key = CHUNKS[c]
                if key[0] == "ada" and key[1] < 2:
                    g = key[1]
                    if g == 0:
                        dve.wait_ge(small_loaded, 16 * N_SMALL)
                    dve.tensor_tensor(gamma8[:, g * C:(g + 1) * C], psum[b][0:N_SEQ, 0:C],
                                      bada8[:, g * C:(g + 1) * C], ALU.add).then_inc(gamma_ready, 1)
                    dve.wait_ge(gamma_ready, g + 1)
                    dve.sem_inc(freed[b], 1)
                    return
                m = MOD_OF[key]
                for ft in range(CT):
                    src, dst = psum[b][:, ft * N_SEQ:(ft + 1) * N_SEQ], modul[:, m, ft, :]
                    if key[0] == "ada":
                        v = V_BADA + CT * key[1] + ft
                        is_scale = key[1] in (ADA["scale1"], ADA["scale2"])
                        ins = dve.tensor_scalar(dst, src, cols[:, v:v + 1], 1.0 if is_scale else 0.0,
                                                ALU.add, ALU.add)
                    else:
                        v = (V_LN1 if key[0] == "tw1" else V_LN2) + ft
                        ins = dve.tensor_scalar(dst, src, 1.0, cols[:, v:v + 1], ALU.add, ALU.mult)
                ins.then_inc(freed[b], 1)

            def norm_stats(kind, n):
                k, s = NM[kind] * 16 + n, seq_of(n)
                dve.wait_ge(*ready_before(kind, n))
                dve.bn_stats(stats[:, k, :], X[:, s, :]).then_inc(stats_mid[kind], 1)
                dve.wait_ge(stats_mid[kind], n + 1)
                dve.bn_aggr(mean_var[:, k, :], stats[:, k, :]).then_inc(stats_ms[kind], 1)
                dve.wait_ge(stats_ms[kind], n + 1)
                if layer_of(n) == 0:
                    dve.tensor_copy(msq[:, k, 0:1], mean_var[:, k, 1:2]).then_inc(stats_ready[kind], 1)
                else:
                    dve.scalar_tensor_tensor(out=msq[:, k, 0:1], in0=mean_var[:, k, 0:1],
                                             scalar=mean_var[:, k, 0:1], in1=mean_var[:, k, 1:2],
                                             op0=ALU.mult, op1=ALU.add).then_inc(stats_ready[kind], 1)

            def norm_apply(kind, n):
                m, k, s = NM[kind], NM[kind] * 16 + n, seq_of(n)
                dve.wait_ge(rstd_ready[kind], n + 1)
                if n >= 2:
                    bb, tt = PLAN[("norm_apply", kind, n - 2)]
                    dve.wait_ge(filled[bb], tt + 1)
                    dve.wait_ge(h_lo_ready[kind], n - 1)
                if layer_of(n) == 0:
                    dve.tensor_scalar(xn[:, m, n % 2, :], X[:, s, :], mean_var[:, k, 0:1], rstd[:, k, :],
                                      ALU.subtract, ALU.mult).then_inc(xn_ready[kind], 1)
                else:
                    dve.tensor_scalar(xn[:, m, n % 2, :], X[:, s, :], rstd[:, k, :], None,
                                      ALU.mult).then_inc(xn_ready[kind], 1)

            def norm_mod(kind, n):
                m, j, s = NM[kind], n % 2, seq_of(n)
                b, t = PLAN[("norm_apply", kind, n)]
                dve.wait_ge(filled[b], t + 1)
                for ft in range(CT):
                    src, dst = psum[b][:, ft * P:(ft + 1) * P], h_full[:, m, j, ft, :]
                    if layer_of(n) == 0:
                        k = 0 if kind == "a" else 2
                        ins = dve.tensor_scalar(dst, src, modul[:, k, ft, s:s + 1], modul[:, k + 1, ft, s:s + 1],
                                                ALU.mult, ALU.add)
                    else:
                        k = 4 if kind == "a" else 5
                        ins = dve.tensor_scalar(dst, src, modul[:, k, ft, s:s + 1], None, ALU.mult)
                ins.then_inc(h_ready[kind], 1)
                dve.wait_ge(h_ready[kind], n + 1)
                dve.sem_inc(freed[b], 1)

            def qk_product(n):
                o, j = ord0(n), n % 2
                b, t = PLAN[("qk_product", n)]
                dve.wait_ge(filled[b], t + 1)
                if o >= 2:
                    dve.wait_ge(qk_squared, o - 1)
                dve.tensor_tensor(qk[:, j, :], psum[b][:, :], qk_bias[:, :], ALU.add).then_inc(qk_ready, 1)
                dve.wait_ge(qk_ready, o + 1)
                dve.sem_inc(freed[b], 1)

            def v_product(n):
                o, j = ord0(n), n % 2
                b, t = PLAN[("v_product", n)]
                dve.wait_ge(filled[b], t + 1)
                if n >= 2:
                    dve.wait_ge(values_summed, 4 * (n - 1))
                pv = psum[b][:, 0:C].rearrange("p (h e d) -> p h e d", e=2, d=D0)
                bv = v_bias[:, :].rearrange("p (h e d) -> p h e d", e=2, d=D0)
                dst = v_pad[:, j, :, :].rearrange("p (h e) w -> p h e w", e=2)
                for e in range(2):
                    ins = dve.tensor_tensor(dst[:, :, e, e * D0:(e + 1) * D0], pv[:, :, e, :], bv[:, :, e, :],
                                            ALU.add)
                ins.then_inc(v_ready, 1)
                dve.wait_ge(v_ready, o + 1)
                dve.sem_inc(freed[b], 1)
                dve.wait_ge(qk_squared, o + 1)
                dve.tensor_reduce(qk_ss[:, j, :], qk_sq[:, j, :].rearrange("p (h d) -> p h d", d=D0), AX_X,
                                  ALU.add).then_inc(qk_summed, 1)
                dve.wait_ge(qk_summed, o + 1)
                if o >= 2:
                    dve.wait_ge(qk_root, o - 1)
                dve.tensor_scalar(qk_fl[:, j, :], qk_ss[:, j, :], NORM_FLOOR, None, ALU.max).then_inc(qk_floor, 1)

            def qk_scale(n):
                o, j = ord0(n), n % 2
                dve.wait_ge(qk_rnorm, o + 1)
                v3 = [t[:, j, :].rearrange("p (h d) -> p h d", d=D0) for t in (qk_n, qk)]
                dve.tensor_tensor(v3[0], v3[1], qk_rs[:, j, :].unsqueeze(2).to_broadcast([P, 2 * H0, D0]),
                                  ALU.mult).then_inc(qk_normed, 1)
                dve.wait_ge(qk_hi_ready, o + 1)
                for s in range(2):
                    ins = dve.tensor_tensor(qk_pack[:, j, s, :, D0:2 * D0],
                                            qk_n[:, j, s * C:(s + 1) * C].rearrange("p (h d) -> p h d", d=D0),
                                            qk_pack[:, j, s, :, 0:D0], ALU.subtract)
                ins.then_inc(qk_lo_ready, 1)

            def qk_turn(n):
                o, j = ord0(n), n % 2
                if n >= 2:
                    dve.wait_ge(exp_ready, 4 * (n - 1))
                b, t = PLAN[("q_turn", n)]
                dve.wait_ge(filled[b], t + 1)
                v = psum[b][:, :].bitcast(F16)
                dve.tensor_copy(qkT[:, j, 0, :, :], v[:, 0:512].rearrange("p (g t) -> p g t", g=4))
                dve.tensor_copy(qkT[:, j, 2, :, :], v[:, 512:1024].rearrange("p (g t) -> p g t", g=4)
                                ).then_inc(freed[b], 1)
                b, t = PLAN[("k_turn", n)]
                dve.wait_ge(filled[b], t + 1)
                dve.tensor_copy(qkT[:, j, 1, :, :], v[:, 0:512].rearrange("p (g t) -> p g t", g=4)
                                ).then_inc(freed[b], 1)

            def rope(n):
                o, j, s = ord1(n), n % 2, seq_of(n)
                b, t = PLAN[("qkv1_product", n)]
                dve.wait_ge(freed[b], t + 1)
                if o == 0:
                    dve.wait_ge(table_ready, 1)
                if o >= 1:
                    dve.wait_ge(rope_ready, o)
                src = qkv1[:, j, 0:C + D1].rearrange("p (h e f) -> p h e f", e=2, f=HALF)
                cs = cos_t[:, s, :].unsqueeze(1).to_broadcast([P, 18, HALF])
                dve.tensor_tensor(rope_c[:, :, :, :].rearrange("p h e f -> p (h e) f"),
                                  qkv1[:, j, 0:C + D1].rearrange("p (h f) -> p h f", f=HALF), cs, ALU.mult)
                for e in range(2):
                    sn = sin_t[:, s, e, :].unsqueeze(1).to_broadcast([P, 9, HALF])
                    ins = dve.tensor_tensor(rope_s[:, :, e, :], src[:, :, 1 - e, :], sn, ALU.mult)
                ins.then_inc(rope_sin, 1)
                dve.wait_ge(rope_sin, o + 1)
                if o >= 2:
                    bb, tt = PLAN[("qk1_turn", of_ord1(o - 2))]
                    dve.wait_ge(filled[bb], tt + 1)
                rc = rope_c[:, :, :, :].rearrange("p h e f -> p h (e f)")
                rs = rope_s[:, :, :, :].rearrange("p h e f -> p h (e f)")
                dve.tensor_tensor(qk1_rot[:, j, 0:H1, :], rc[:, 0:H1, :], rs[:, 0:H1, :], ALU.add)
                dve.tensor_tensor(qk1_rot[:, j, H1:H1 + 4, :], rc[:, H1:H1 + 1, :].to_broadcast([P, 4, D1]),
                                  rs[:, H1:H1 + 1, :].to_broadcast([P, 4, D1]), ALU.add).then_inc(rope_ready, 1)

            def qk1_turn(n):
                j = n % 2
                b, t = PLAN[("qk1_turn", n)]
                if n >= 2:
                    dve.wait_ge(exp_ready, 4 * (n - 1))
                dve.wait_ge(filled[b], t + 1)
                dve.tensor_copy(qk1T[:, j, :, :], psum[b][:, 0:3 * P].rearrange("p (g t) -> p g t", g=3)
                                ).then_inc(freed[b], 1)

            def softmax(G):
                n, U = G // 4, len(heads_of(G))
                b, t = PLAN[("scores", G)]
                dve.wait_ge(filled[b], t + 1)
                S = psum[b][:, 0:U * P].rearrange("p (u k) -> p u k", u=U)
                if G >= 2:
                    dve.wait_ge(exp_ready, G - 1)
                    dve.wait_ge(filled["probs"], G - 1)
                if layer_of(n) == 0:
                    dve.tensor_tensor(z[:, G % 2, :, :], S, bias_mask[:, :].unsqueeze(1).to_broadcast([P, U, P]),
                                      ALU.add).then_inc(z_ready, 1)
                    dve.wait_ge(z_ready, 4 * ord0(n) + G % 4 + 1)
                    dve.sem_inc(freed[b], 1)
                    dve.tensor_reduce(neg_max[:, G % 2, 0:U], z[:, G % 2, :, :], AX_X, ALU.max,
                                      negate=True).then_inc(max_ready, 1)
                else:
                    dve.tensor_reduce(neg_max[:, G % 2, 0:U], S, AX_X, ALU.max, negate=True).then_inc(max_mid, 1)
                    dve.wait_ge(max_mid, 4 * ord1(n) + G % 4 + 1)
                    dve.tensor_scalar(neg_max_s[:, G % 2, 0:U], neg_max[:, G % 2, 0:U], SCORE_SCALE1, None,
                                      ALU.mult).then_inc(max_ready, 1)

            def turn_probs(G):
                if layer_of(G // 4) == 1:
                    sb_, _ = PLAN[("scores", G)]
                    dve.wait_ge(exp_ready, G + 1)
                    dve.sem_inc(freed[sb_], 1)
                if G % 2 == 1:
                    return
                b, t = PLAN[("turn_probs", G)]
                U = len(heads_of(G))
                dve.wait_ge(filled[b], t + 1)
                if G >= 2:
                    dve.wait_ge(values_summed, G - 1)
                dve.tensor_copy(probsT[:, G % 2, 0:U, :], psum[b][:, 0:U * P].rearrange("p (u q) -> p u q", u=U)
                                ).then_inc(freed[b], 1)

            def attn_out(n):
                b, t = PLAN[("output", n)]
                dve.wait_ge(values_summed, 4 * n + 4)
                v = psum[b][:, :].rearrange("p (t s q) -> p t s q", t=CT, s=2)
                dve.reciprocal(rden[:, :, :], v[:, :, 1, :]).then_inc(rden_ready, 1)
                dve.wait_ge(rden_ready, n + 1)
                if n >= 2:
                    dve.wait_ge(o_used, n - 1)
                dve.tensor_tensor(o_full[:, n % 2, :, :], v[:, :, 0, :], rden[:, :, :], ALU.mult
                                  ).then_inc(o_ready, 1)
                dve.wait_ge(o_ready, n + 1)
                dve.sem_inc(freed[b], 1)

            def residual(kind, key, n):
                b, t = PLAN[(key, n)]
                m, s, o = NM[kind], seq_of(n), ord0(n)
                dve.wait_ge(filled[b], t + 1)
                if layer_of(n) == 1:
                    dve.tensor_tensor(X[:, s, :], psum[b][:, 0:C], X[:, s, :], ALU.add).then_inc(res_ready[kind], 1)
                    dve.wait_ge(res_ready[kind], n + 1)
                    dve.sem_inc(freed[b], 1)
                    return
                pair = ROUNDS[n // 2][0]
                dve.wait_ge(small_loaded, 16 * N_SMALL)
                dve.tensor_tensor(res_t[:, m, 0, :], psum[b][:, 0:C], res_bias[:, m, :], ALU.add
                                  ).then_inc(res_mid[kind], 1)
                dve.wait_ge(res_mid[kind], o + 1)
                dve.sem_inc(freed[b], 1)
                dve.wait_ge(gamma_loaded[pair], 32)
                if n >= 1:
                    dve.wait_ge(res_ready[kind], n)
                dve.tensor_tensor(res_t[:, m, 1, :], res_t[:, m, 0, :], gamma[:, pair % 2, n % 2, m * C:(m + 1) * C],
                                  ALU.mult).then_inc(res_scaled[kind], 1)

            def gelu(r, c):
                o, m = fc_ord(r, c), mlp_ord(r, c)
                dve.wait_ge(g_poly, o + 1)
                dve.tensor_tensor(g_a[:, o % 2, :], g_b[:, o % 2, :], g_u[:, o % 2, :], ALU.mult
                                  ).then_inc(g_inner, 1)
                dve.wait_ge(g_tanh, m + 1)
                if c == 0 and r >= 1:
                    dve.wait_ge(g_used, r)
                dve.scalar_tensor_tensor(out=g_h[:, 2 * c:2 * c + 2, :].rearrange("p f t -> p (f t)"),
                                         in0=g_a[:, o % 2, :], scalar=1.0, in1=g_u[:, o % 2, :],
                                         op0=ALU.add, op1=ALU.mult).then_inc(g_full, 1)

            def gate_up(r, f):
                m = mlp_ord(r, f)
                b, t = PLAN[("gate_up", r, f)]
                dve.wait_ge(g_tanh, m + 1)
                dve.scalar_tensor_tensor(out=g_b[:, f % 2, 0:256], in0=g_a[:, f % 2, 0:256], scalar=1.0,
                                         in1=psum[b][:, 0:256], op0=ALU.add, op1=ALU.mult).then_inc(g_gated, 1)
                dve.wait_ge(g_gated, gu_ord(r, f) + 1)
                if f == 0 and r >= 1:
                    dve.wait_ge(g_used, r)
                dve.scalar_tensor_tensor(out=g_h[:, f, :], in0=g_b[:, f % 2, 0:256], scalar=0.5,
                                         in1=psum[b][:, 256:512], op0=ALU.mult, op1=ALU.mult).then_inc(g_full, 1)
                dve.wait_ge(g_full, m + 1)
                dve.sem_inc(freed[b], 1)

            for step in SCHEDULE:
                k, a = step[0], step[1:]
                if k == "conditioning":
                    conditioning()
                elif k == "rope_tables":
                    rope_tables()
                elif k == "prepare":
                    prepare(*a)
                elif k == "modulation":
                    modulation(*a)
                elif k == "norm_stats":
                    norm_stats(*a)
                elif k == "norm_apply":
                    norm_apply(*a)
                elif k == "norm_mod":
                    norm_mod(*a)
                elif k == "qk_product":
                    qk_product(*a)
                elif k == "v_product":
                    v_product(*a)
                elif k == "qk_scale":
                    qk_scale(*a)
                elif k == "qk_turn":
                    qk_turn(*a)
                elif k == "rope":
                    rope(*a)
                elif k == "qk1_turn":
                    qk1_turn(*a)
                elif k == "softmax":
                    softmax(*a)
                elif k == "turn_probs":
                    turn_probs(*a)
                elif k == "attn_out":
                    attn_out(*a)
                elif k == "project":
                    residual("a", "project", *a)
                elif k == "down":
                    residual("m", "down", *a)
                elif k == "gelu":
                    gelu(*a)
                elif k == "gate_up":
                    gate_up(*a)

        @block.tensor
        def _(pe):
            def take(key):
                b, t = PLAN[key]
                if t >= 1:
                    pe.wait_ge(freed[b], t)
                return psum[b], filled[b]

            def product3(dst, parts, start=True, stop=True):
                last = len(parts) - 1
                for i, (sh, sl, mh, ml) in enumerate(parts):
                    pe.matmul(dst, sh, mh, start=start and i == 0, stop=False)
                    pe.matmul(dst, sh, ml, start=False, stop=False)
                    ins = pe.matmul(dst, sl, mh, start=False, stop=stop and i == last)
                return ins

            def conditioning():
                bank, full = take(("conditioning",))
                pe.wait_ge(consts_set, 1)
                pe.wait_ge(vec_loaded, 16 * 5)
                pe.wait_ge(cond_silu, 1)
                for s, src in enumerate((silu8, cond8)):
                    for ct in range(CT):
                        at = (s * CT + ct) * N_SEQ
                        pe.transpose(bank[:, at:at + N_SEQ], src[:, ct * P:(ct + 1) * P], ident[0:N_SEQ, 0:N_SEQ])
                pe.transpose(bank[:, V0:V0 + N_VEC], vec_rows[:, :], ident[0:N_VEC, 0:N_VEC]).then_inc(full, 1)

            def prepare(c):
                name, i = CHUNKS[c]
                bank, full = take(("prepare", c))
                if c == 0:
                    pe.wait_ge(consts_set, 1)
                extra = sum(1 for q in range(c % STAGE, c + 1, STAGE) if CHUNKS[q][0] == "Wkv")
                pe.wait_ge(stage_loaded[c % STAGE], 16 * (c // STAGE + 1 + extra))
                raw = stage[:, c % STAGE, :]
                if name == "Wkv":
                    for ct in range(CT):
                        ins = pe.transpose(bank[:, ct * 2 * D1:(ct + 1) * 2 * D1],
                                           raw[0:2 * D1, ct * P:(ct + 1) * P], ident[0:2 * D1, 0:2 * D1])
                elif name in WIDE:
                    for ct in range(4):
                        ins = pe.transpose(bank[:, ct * P:(ct + 1) * P], raw[:, ct * P:(ct + 1) * P], ident[:, :])
                else:
                    for ct in range(CT):
                        for rt in range(2):
                            ins = pe.transpose(bank[:, (2 * ct + rt) * P:(2 * ct + rt + 1) * P],
                                               raw[:, rt * C + ct * P:rt * C + (ct + 1) * P], ident[:, :])
                ins.then_inc(full, 1)
                pe.wait_ge(full, PLAN[("prepare", c)][1] + 1)
                pe.sem_inc(weights_turned, 1)

            def modulation(c):
                key, o = CHUNKS[c], IS_ADA[c]
                bank, full = take(("modulation", c))
                pe.wait_ge(weight_ready, c + 1)
                if o == 0:
                    pe.wait_ge(freed["turn"], 1)
                wt = adaT[:, o % 2, :, :]
                base = 0 if key[0] == "ada" else CT * N_SEQ
                cT = [cols[:, base + ct * N_SEQ:base + (ct + 1) * N_SEQ] for ct in range(CT)]
                if key[0] == "ada" and key[1] < 2:
                    for ct in range(CT):
                        ins = pe.matmul(bank[0:N_SEQ, 0:C], cT[ct], wt[:, ct, :], start=(ct == 0),
                                        stop=(ct == CT - 1))
                else:
                    for ft in range(CT):
                        for ct in range(CT):
                            ins = pe.matmul(bank[:, ft * N_SEQ:(ft + 1) * N_SEQ], wt[:, ct, ft * P:(ft + 1) * P],
                                            cT[ct], start=(ct == 0), stop=(ct == CT - 1))
                ins.then_inc(full, 1)
                pe.wait_ge(full, PLAN[("modulation", c)][1] + 1)
                pe.sem_inc(ada_used, 1)

            def norm_apply(kind, n):
                bank, full = take(("norm_apply", kind, n))
                pe.wait_ge(xn_ready[kind], n + 1)
                for ft in range(CT):
                    ins = pe.transpose(bank[:, ft * P:(ft + 1) * P], xn[:, NM[kind], n % 2, ft * P:(ft + 1) * P],
                                       ident[:, :])
                ins.then_inc(full, 1)

            def token_major(key, n, wname, lo_col, width):
                bank, full = take(key)
                j = n % 2
                hi, lo = WT[wname]
                parts = [(h_hi[:, 0, ct, j * P:(j + 1) * P], h_lo[:, 0, ct, j * P:(j + 1) * P],
                          hi[:, ct, lo_col:lo_col + width], lo[:, ct, lo_col:lo_col + width]) for ct in range(CT)]
                return product3(bank[:, 0:width], parts), full

            def qk_product(n):
                pe.wait_ge(h_lo_ready["a"], n + 1)
                pe.wait_ge(weight_ready, LAST_CHUNK["Wqkv"] + 1)
                ins, full = token_major(("qk_product", n), n, "Wqkv", 0, 2 * C)
                ins.then_inc(full, 1)

            def v_product(n):
                ins, full = token_major(("v_product", n), n, "Wqkv", 2 * C, C)
                ins.then_inc(full, 1)
                if n % 2 == 1:
                    pe.wait_ge(full, PLAN[("v_product", n)][1] + 1)
                    pe.sem_inc(h_used["a"], 1)

            def qkv1_product(n):
                pe.wait_ge(h_lo_ready["a"], n + 1)
                pe.wait_ge(weight_ready, LAST_CHUNK["Wkv"] + 1)
                ins, full = token_major(("qkv1_product", n), n, "Wqkv1", 0, QKV1)
                ins.then_inc(full, 1)
                if n % 2 == 1:
                    pe.wait_ge(full, PLAN[("qkv1_product", n)][1] + 1)
                    pe.sem_inc(h_used["a"], 1)

            def qk_turn(n):
                j = n % 2
                pe.wait_ge(qk_packed, ord0(n) + 1)
                pe.wait_ge(consts_set, 2)
                for key, slabs in ((("q_turn", n), (0, 2)), (("k_turn", n), (1,))):
                    bank, full = take(key)
                    v = bank[:, :].bitcast(F16)
                    for i, s in enumerate(slabs):
                        for g in range(4):
                            at = i * 512 + g * P
                            ins = pe.transpose(v[:, at:at + P],
                                               qk_pack[:, j, s, 4 * g:4 * g + 4, :].rearrange("p h d -> p (h d)"),
                                               ident16[:, :])
                    ins.then_inc(full, 1)
                pe.wait_ge(full, PLAN[("k_turn", n)][1] + 1)
                pe.sem_inc(qk_turned, 1)

            def qk1_turn(n):
                j = n % 2
                pe.wait_ge(rope_ready, ord1(n) + 1)
                bank, full = take(("qk1_turn", n))
                for g in range(3):
                    ins = pe.transpose(bank[:, g * P:(g + 1) * P],
                                       qk1_rot[:, j, 4 * g:4 * g + 4, :].rearrange("p h d -> p (h d)"), ident[:, :])
                ins.then_inc(full, 1)

            def scores(G):
                n, i, j = G // 4, G % 4, (G // 4) % 2
                bank, full = take(("scores", G))
                rows = slice(QUAD * i, QUAD * (i + 1))
                if i == 0:
                    b, t = PLAN[("k_turn", n) if layer_of(n) == 0 else ("qk1_turn", n)]
                    pe.wait_ge(freed[b], t + 1)
                for u, h in enumerate(heads_of(G)):
                    dst, g = bank[:, u * P:(u + 1) * P], h // 4
                    if layer_of(n) == 0:
                        pe.matmul(dst, qkT[rows, j, 0, g, :], qkT[rows, j, 1, g, :], start=True, stop=False)
                        ins = pe.matmul(dst, qkT[rows, j, 2, g, :], qkT[rows, j, 1, g, :], start=False, stop=True)
                    else:
                        ins = pe.matmul(dst, qk1T[rows, j, g, :], qk1T[rows, j, 2, :], start=True, stop=True)
                ins.then_inc(full, 1)

            def turn_probs(G):
                bank, full = take(("turn_probs", G))
                pe.wait_ge(exp_ready, G + 1)
                for u in range(len(heads_of(G))):
                    ins = pe.transpose(bank[:, u * P:(u + 1) * P], probs[:, G % 2, u, :], ident[:, :])
                ins.then_inc(full, 1)

            def values(G):
                n, i, j = G // 4, G % 4, (G // 4) % 2
                b, t = PLAN[("output", n)]
                bank = psum[b]
                if i == 0 and t >= 1:
                    pe.wait_ge(freed[b], t)
                if i == 0 and layer_of(n) == 0:
                    pe.wait_ge(v_ready, ord0(n) + 1)
                pb, pt = PLAN[("turn_probs", G)]
                pe.wait_ge(freed[pb], pt + 1)
                for u, h in enumerate(heads_of(G)):
                    if layer_of(n) == 0:
                        tile, quad, even = h // 8, (h % 8) // 2, h % 2 == 0
                        stat, ones = v_pad[:, j, h, :], ones_half[:, h % 2, :]
                        fresh = even and tile == 0
                    else:
                        tile, quad = h // 4, h % 4
                        stat, ones = qkv1[:, j, C + D1:QKV1], ones_quad[:, :]
                        fresh = tile == 0
                    rows = slice(QUAD * quad, QUAD * (quad + 1))
                    at = tile * 2 * P
                    done = layer_of(n) == 1 or not even
                    pe.matmul(bank[rows, at:at + P], stat, probsT[:, G % 2, u, :], start=fresh, stop=done,
                              skip_group_check=True)
                    ins = pe.matmul(bank[rows, at + P:at + 2 * P], ones, probsT[:, G % 2, u, :], start=False,
                                    stop=done, skip_group_check=True)
                ins.then_inc(values_summed, 1)

            def project(n):
                j = n % 2
                bank, full = take(("project", n))
                pe.wait_ge(o_ready, n + 1)
                name = "Wproj" if layer_of(n) == 0 else "Wo"
                pe.wait_ge(weight_ready, LAST_CHUNK[name] + 1)
                for ct in range(CT):
                    ins = pe.matmul(bank[:, 0:C], o_full[:, j, ct, :], WT1[name][:, ct, :], start=(ct == 0),
                                    stop=(ct == CT - 1))
                ins.then_inc(full, 1)
                pe.wait_ge(full, PLAN[("project", n)][1] + 1)
                pe.sem_inc(o_used, 1)

            def hidden(key, r, names, cols_of):
                bank, full = take(key)
                for s, (name, f) in enumerate(zip(names, cols_of)):
                    hi, lo = WT[name]
                    ins = product3(bank[:, s * 256:(s + 1) * 256],
                                   [(hi[:, ct, f * P:(f + 1) * P], lo[:, ct, f * P:(f + 1) * P],
                                     h_hi[:, 1, ct, :], h_lo[:, 1, ct, :]) for ct in range(CT)])
                ins.then_inc(full, 1)
                return full

            def fc1(r, c):
                if c == 0:
                    pe.wait_ge(h_lo_ready["m"], 2 * r + 2)
                    pe.wait_ge(weight_ready, LAST_CHUNK["Wfc1"] + 1)
                full = hidden(("fc1", r, c), r, ("Wfc1", "Wfc1"), (2 * c, 2 * c + 1))
                if c == FT // 2 - 1:
                    pe.wait_ge(full, PLAN[("fc1", r, c)][1] + 1)
                    pe.sem_inc(h_used["m"], 1)

            def gate_up(r, f):
                if f == 0:
                    pe.wait_ge(h_lo_ready["m"], 2 * r + 2)
                pe.wait_ge(weight_ready, CHUNK_AT[("Wu", 2 * (f // 2))] + 1)
                full = hidden(("gate_up", r, f), r, ("Wg", "Wu"), (f, f))
                if f == FT - 1:
                    pe.wait_ge(full, PLAN[("gate_up", r, f)][1] + 1)
                    pe.sem_inc(h_used["m"], 1)

            def down(n):
                j, r = n % 2, n // 2
                bank, full = take(("down", n))
                name = "Wfc2" if layer_of(n) == 0 else "Wd"
                pe.wait_ge(weight_ready, LAST_CHUNK[name] + 1)
                for f in range(FT):
                    if j == 0:
                        pe.wait_ge(g_full, mlp_ord(r, f // 2 if layer_of(n) == 0 else f) + 1)
                    ins = pe.matmul(bank[:, 0:C], g_h[:, f, j * P:(j + 1) * P], WT1[name][:, f, :],
                                    start=(f == 0), stop=(f == FT - 1))
                ins.then_inc(full, 1)
                if j == 1:
                    pe.wait_ge(full, PLAN[("down", n)][1] + 1)
                    pe.sem_inc(g_used, 1)

            for step in SCHEDULE:
                k, a = step[0], step[1:]
                if k == "conditioning":
                    conditioning()
                elif k == "prepare":
                    prepare(*a)
                elif k == "modulation":
                    modulation(*a)
                elif k == "norm_apply":
                    norm_apply(*a)
                elif k == "qk_product":
                    qk_product(*a)
                elif k == "v_product":
                    v_product(*a)
                elif k == "qkv1_product":
                    qkv1_product(*a)
                elif k == "qk_turn":
                    qk_turn(*a)
                elif k == "qk1_turn":
                    qk1_turn(*a)
                elif k == "scores":
                    scores(*a)
                elif k == "turn_probs":
                    turn_probs(*a)
                elif k == "values":
                    values(*a)
                elif k == "project":
                    project(*a)
                elif k == "fc1":
                    fc1(*a)
                elif k == "gate_up":
                    gate_up(*a)
                elif k == "down":
                    down(*a)


NAMES = {"Wqkv": "L0_cond_Wqkv", "q_bias": "L0_cond_q_bias", "v_bias": "L0_cond_v_bias",
         "sml": "L0_cond_scale_mul_log", "Wproj": "L0_cond_Wproj", "bproj": "L0_cond_bproj",
         "Wada": "L0_cond_Wada", "bada": "L0_cond_bada", "Wfc1": "L0_cond_Wfc1", "bfc1": "L0_cond_bfc1",
         "Wfc2": "L0_cond_Wfc2", "bfc2": "L0_cond_bfc2", "ln1_w": "L1_cond_ln1_w", "tw1": "L1_cond_ln1_tw",
         "ln2_w": "L1_cond_ln2_w", "tw2": "L1_cond_ln2_tw", "Wq": "L1_cond_Wq", "Wk": "L1_cond_Wk",
         "Wv": "L1_cond_Wv", "Wo": "L1_cond_Wo", "Wg": "L1_cond_Wg", "Wu": "L1_cond_Wu", "Wd": "L1_cond_Wd"}


def kernel(**inputs):
    import numpy as _np
    import concourse.bacc as _bacc
    from concourse import mybir as _mybir
    from concourse.bass_utils import run_bass_kernel_spmd as _run

    nc = _bacc.Bacc("TRN2", target_bir_lowering=False, num_devices=1)
    arrays = {}

    def declare(name, shape=None, turned=False):
        a = _np.asarray(inputs[name])
        a = _np.ascontiguousarray(a.T if turned else a)
        if shape is not None:
            a = a.reshape(shape)
        arrays[f"in_{name}"] = a
        return nc.dram_tensor(f"in_{name}", a.shape, _mybir.dt.from_np(a.dtype), kind="ExternalInput").ap()

    x = declare("x")
    cond = declare("cond_2048")
    pos = declare("pos_BxS", turned=True)
    mask = declare("mask_1x1xSxS_ff0", (P, P))
    w = {k: declare(v, (H0,) if k == "sml" else None) for k, v in NAMES.items()}
    out = nc.dram_tensor("out", (N_SEQ, P, C), _mybir.dt.float32, kind="ExternalOutput").ap()
    build(nc, x, cond, pos, mask, w, out)
    r = _run(nc, [arrays], core_ids=[0])
    return r.results[0]["out"]
```

```python
from contextlib import ExitStack

import numpy as np

import concourse.bass as bass
from concourse import mybir

F32 = mybir.dt.float32
F32R = mybir.dt.float32r
F16 = mybir.dt.float16
I32 = mybir.dt.int32
ALU = mybir.AluOpType
ACT = mybir.ActivationFunctionType
AX_X = mybir.AxisListType.X

P = 128
N_SEQ, C, HID = 8, 256, 1024
PAIRS = N_SEQ // 2
CT = C // P
FT = HID // P
H0, D0 = 16, 16
H1, D1 = 8, 32
QUAD = 32
QKV1 = C + 2 * D1
LN_EPS = 1e-6
NORM_FLOOR = 1e-24
MAX_LOG_SCALE = float(np.log(np.float32(100.0)))
GELU_C = float(np.sqrt(2.0 / np.pi).astype(np.float32))
SCORE_SCALE1 = float(1.0 / np.sqrt(np.float32(D1)))
ROUND_MAGIC = 1.5 * 2.0 ** 23
TWO_PI = 2.0 * np.pi
PI_1 = 6.28125
PI_2 = float(np.float32(np.floor((TWO_PI - PI_1) * 2 ** 21) / 2 ** 21))
PI_3 = float(np.float32(TWO_PI - PI_1 - PI_2))
SIN_LIMIT = 3.1415925

ROUNDS = [(0, 0), (1, 0), (0, 1), (1, 1), (2, 0), (3, 0), (2, 1), (3, 1)]
ROUND_OF = {pl: r for r, pl in enumerate(ROUNDS)}
STAGE = 5

ADA = {"gamma1": 0, "gamma2": 1, "scale1": 2, "scale2": 3, "shift1": 4, "shift2": 5}
WIDE = ("Wfc2", "Wd")
CHUNKS = ([("ada", ADA["scale1"]), ("ada", ADA["shift1"])]
          + [("Wqkv", 2 * i) for i in range(3)]
          + [("ada", ADA["gamma1"]), ("ada", ADA["gamma2"]), ("Wproj", 0),
             ("ada", ADA["scale2"]), ("ada", ADA["shift2"]), ("tw1", 0), ("tw2", 0)]
          + [("Wfc1", 2 * i) for i in range(4)]
          + [("Wfc2", i) for i in range(4)]
          + [("Wq", 0), ("Wkv", 0), ("Wo", 0)]
          + [(w, 2 * i) for i in range(4) for w in ("Wg", "Wu")]
          + [("Wd", i) for i in range(4)])
N_CHUNKS = len(CHUNKS)
CHUNK_AT = {c: i for i, c in enumerate(CHUNKS)}
IS_ADA = {i: n for n, i in enumerate(i for i, c in enumerate(CHUNKS) if c[0] in ("ada", "tw1", "tw2"))}
LAST_CHUNK = {}
for _i, _c in enumerate(CHUNKS):
    LAST_CHUNK[_c[0]] = _i
WHOLE = ("Wproj", "Wo", "Wfc2", "Wd")
SLOT, START, GROUP_US = 34.0, 8.0, 2.6


def CHUNK_DUE(c):
    return -5 + 0.3 * c if c < 5 else START + 1.6 * (c - 5)


MOD_OF = {("ada", 2): 0, ("ada", 4): 1, ("ada", 3): 2, ("ada", 5): 3, ("tw1", 0): 4, ("tw2", 0): 5}


BANK_KINDS = {"turn": ["turn"], "linear": ["linear"], "hidden": ["hidden0", "hidden1"],
              "scores": ["scores0", "scores1"], "probs": ["probs"], "output": ["output"]}
BANKS = [b for kind in BANK_KINDS.values() for b in kind]
WAKE = 0.12


def seq_of(n):
    return 2 * ROUNDS[n // 2][0] + n % 2


def layer_of(n):
    return ROUNDS[n // 2][1]


def heads_of(group):
    i = group % 4
    tiles = H0 // 4 if layer_of(group // 4) == 0 else H1 // 4
    return [4 * g + i for g in range(tiles)]


def list_steps():
    steps = {}

    def add(key, engine, us, after=(), fills=None, frees=None, at=0.0):
        steps[key] = (engine, us, [k for k in after if k is not None], fills, frees, at)

    def prev(key, n, back=1, first=0):
        return key + (n - back,) if n - back >= first else None

    n_rounds = len(ROUNDS)
    add(("cond_tanh",), "ACT", 2.5, at=-9)
    add(("cond_silu",), "DVE", 0.7, [("cond_tanh",)], at=-9)
    add(("cond_turn",), "PE", 0.8, [("cond_silu",)], "turn", at=-9)
    add(("cond_copy",), "DVE", 0.2, [("cond_turn",)], frees=("cond_turn",), at=-9)
    add(("angles",), "DVE", 2.5, [("cond_silu",)], at=2)
    add(("sines",), "ACT", 3.0, [("angles",)], at=2)
    for c in range(N_CHUNKS):
        due = CHUNK_DUE(c)
        add(("load", c), "SP", 1.3, [prev(("load",), c), ("weight_turn", c - STAGE) if c >= STAGE else None], at=due)
        add(("weight_turn", c), "PE", 0.45, [("load", c), prev(("weight_turn",), c)], "hidden", at=due)
        if c in IS_ADA:
            o = IS_ADA[c]
            users = [("modulate", q) for q in IS_ADA if IS_ADA[q] == o - 2]
            add(("weight_low", c), "DVE", 0.65, [("weight_turn", c), prev(("weight_low",), c)] + users,
                frees=("weight_turn", c), at=due)
            add(("modulate", c), "PE", 0.5, [("weight_low", c), ("cond_copy",)]
                + [("modulate", q) for q in IS_ADA if IS_ADA[q] == o - 1], "turn", at=due)
            add(("modulated", c), "DVE", 0.3, [("modulate", c)], frees=("modulate", c), at=due)
        elif CHUNKS[c][0] in WHOLE:
            add(("weight_low", c), "DVE", 0.65, [("weight_turn", c), prev(("weight_low",), c)],
                frees=("weight_turn", c), at=due)
        else:
            add(("weight_high", c), "ACT", 0.55, [("weight_turn", c)]
                + [("weight_high", q) for q in range(c) if ("weight_high", q) in steps][-1:], at=due)
            add(("weight_low", c), "DVE", 0.65, [("weight_high", c), prev(("weight_low",), c)],
                frees=("weight_turn", c), at=due)
    g2 = CHUNK_AT[("ada", ADA["gamma2"])]
    add(("gamma_store",), "SP", 2.0, [("modulated", g2)], at=CHUNK_DUE(g2))

    last_of = {}

    def norm(kind, r, at, products):
        pair, layer = ROUNDS[r]
        for j in range(2):
            n = 2 * r + j
            if kind == "m":
                src = [("residual", "a", n)] + ([("residual_add", "a", n)] if layer == 0 else [])
            elif layer == 1:
                q = 2 * ROUND_OF[(pair, 0)] + j
                src = [("residual_add", "m", q)]
            else:
                src = []
            a = at + 0.5 * j
            add(("norm_stats", kind, n), "DVE", 0.75, src + [prev(("norm_stats", kind), n)], at=a)
            add(("norm_root", kind, n), "Pool", 0.9, [("norm_stats", kind, n), prev(("norm_root", kind), n)], at=a)
            add(("norm_apply", kind, n), "DVE", 0.3, [("norm_root", kind, n), prev(("norm_apply", kind), n),
                                                     prev(("norm_low", kind), n, 2)], at=a)
            last = CHUNK_AT[("ada", ADA["shift1"])] if kind == "a" else CHUNK_AT[("ada", ADA["shift2"])]
            if layer == 1:
                last = CHUNK_AT[("tw1" if kind == "a" else "tw2", 0)]
            add(("norm_turn", kind, n), "PE", 0.3, [("norm_apply", kind, n), prev(("norm_turn", kind), n),
                                                   ("modulated", last)], "turn", at=a)
            add(("norm_mod", kind, n), "DVE", 0.65, [("norm_turn", kind, n), prev(("norm_mod", kind), n)], frees=("norm_turn", kind, n), at=a)
            add(("norm_high", kind, n), "ACT", 0.35, [("norm_mod", kind, n), prev(("norm_high", kind), n)]
                + list(last_of.get(kind, [])), at=a)
            add(("norm_low", kind, n), "Pool", 0.7, [("norm_high", kind, n), prev(("norm_low", kind), n)], at=a)
        last_of[kind] = products

    last_j = {}
    for r, (pair, layer) in enumerate(ROUNDS):
        base = SLOT * r + START
        ns = (2 * r, 2 * r + 1)
        prod = [("v_product", n) for n in ns] if layer == 0 else [("qkv1_product", n) for n in ns]
        norm("a", r, base, prod)
        for j, n in enumerate(ns):
            a = base + 2 + 1.0 * j
            old = n - 2
            exps = ("exp", 4 * old + 3) if old >= 0 else None
            if layer == 0:
                w_ready = ("weight_low", LAST_CHUNK["Wqkv"])
                add(("qk_product", n), "PE", 1.3, [("norm_low", "a", n), w_ready], "linear", at=a)
                add(("qk_copy", n), "DVE", 0.65, [("qk_product", n), last_j.get(("qk", j))], frees=("qk_product", n),
                    at=a)
                add(("qk_square", n), "ACT", 0.5, [("qk_copy", n), last_j.get(("pack", j))], at=a)
                add(("v_product", n), "PE", 0.65, [("norm_low", "a", n), ("qk_product", n)], "linear", at=a + 0.1)
                add(("v_copy", n), "DVE", 0.55, [("v_product", n), ("values", 4 * old + 3) if old >= 0 else None],
                    frees=("v_product", n), at=a)
                add(("qk_sum", n), "DVE", 0.75, [("qk_square", n)], at=a)
                add(("qk_root", n), "Pool", 3.2, [("qk_sum", n), ("sines",)], at=a)
                add(("qk_scale", n), "DVE", 0.65, [("qk_root", n)], at=a)
                add(("qk_high", n), "ACT", 0.5, [("qk_scale", n), last_j.get(("kt", j))], at=a)
                add(("qk_low", n), "DVE", 0.7, [("qk_high", n)], at=a)
                add(("qk_swap", n), "Pool", 1.0, [("qk_low", n)], at=a)
                add(("q_turn", n), "PE", 0.85, [("qk_swap", n)], "turn", at=a)
                add(("q_copy", n), "DVE", 0.75, [("q_turn", n), exps], frees=("q_turn", n), at=a)
                add(("k_turn", n), "PE", 0.45, [("q_turn", n)], "turn", at=a)
                add(("k_copy", n), "DVE", 0.35, [("k_turn", n), exps], frees=("k_turn", n), at=a)
                last_j[("qk", j)], last_j[("pack", j)], last_j[("kt", j)] = (("qk_scale", n), ("qk_low", n),
                                                                              ("k_turn", n))
                ready = ("k_copy", n)
            else:
                add(("qkv1_product", n), "PE", 0.85, [("norm_low", "a", n), ("weight_low", LAST_CHUNK["Wkv"])],
                    "linear", at=a)
                add(("qkv1_copy", n), "ACT", 0.4, [("qkv1_product", n), last_j.get(("rope", j)),
                                                  ("values", 4 * old + 3) if old >= 0 else None],
                    frees=("qkv1_product", n), at=a)
                add(("rope", n), "DVE", 1.5, [("qkv1_copy", n), ("sines",), last_j.get(("turn1", j))], at=a)
                add(("qk1_turn", n), "PE", 0.35, [("rope", n)], "turn", at=a)
                add(("qk1_copy", n), "DVE", 0.5, [("qk1_turn", n), exps], frees=("qk1_turn", n), at=a)
                last_j[("rope", j)], last_j[("turn1", j)] = ("rope", n), ("qk1_turn", n)
                ready = ("qk1_copy", n)
            for i in range(4):
                G = 4 * n + i
                g = base + 5 + GROUP_US * (4 * j + i)
                big = layer == 0
                add(("scores", G), "PE", 0.45 if big else 0.57, [ready, prev(("scores",), G)], "scores", at=g)
                add(("row_max", G), "DVE", 1.35 if big else 0.5,
                    [("scores", G), prev(("row_max",), G), prev(("exp",), G, 2), prev(("probs_turn",), G, 2)],
                    frees=("scores", G) if big else None, at=g)
                add(("exp", G), "ACT", 1.4 if big else 0.7, [("row_max", G), prev(("exp",), G)],
                    frees=None if big else ("scores", G), at=g)
                add(("row_inverse", G), "DVE", 0.12, [("exp", G), prev(("row_inverse",), G)], at=g)
                add(("norm_probs", G), "Pool", 1.4 if big else 0.8, [("row_inverse", G), prev(("norm_probs",), G)],
                    at=g)
                add(("probs_turn", G), "PE", 0.43 if big else 0.22, [("norm_probs", G), prev(("probs_turn",), G)],
                    "probs", at=g)
                add(("probs_copy", G), "ACT", 0.5 if big else 0.3,
                    [("probs_turn", G), prev(("probs_copy",), G), prev(("values",), G, 2)],
                    frees=("probs_turn", G), at=g)
                add(("values", G), "PE", 0.4 if big else 0.2, [("probs_copy", G), prev(("values",), G)]
                    + ([("v_copy", n)] if big else []), "output" if i == 0 else None, at=g)
            g = base + 5 + GROUP_US * (4 * j + 3)
            add(("attn_copy", n), "ACT", 0.4, [("values", 4 * n + 3), prev(("project",), n, 2)],
                frees=("values", 4 * n), at=g)
            add(("project", n), "PE", 0.85, [("attn_copy", n), ("weight_low", LAST_CHUNK["Wproj" if layer == 0 else
                                             "Wo"]), prev(("project",), n)], "linear", at=g)
            add(("residual", "a", n), "DVE", 0.7 if layer == 0 else 0.35, [("project", n), prev(("residual", "a"), n)]
                + ([("gamma_load", pair)] if layer == 0 else [])
                + ([("residual_add", "a", q) for q in (n - 1,) if ("residual_add", "a", q) in steps]),
                frees=("project", n), at=g)
            if layer == 0:
                add(("residual_add", "a", n), "Pool", 0.7, [("residual", "a", n)], at=g)
        base = SLOT * (r + 1) + START
        chunks = FT // 2 if layer == 0 else FT
        names = ["fc1" if layer == 0 else "gate_up"]
        norm("m", r, base - 3, [(names[0], r, chunks - 1)])
        down_before = [("down", 2 * r - 1)] if r else []
        for c in range(chunks):
            a = base + c * (SLOT - 4) * 0.6 / chunks
            key = (names[0], r, c)
            o = [(k, q, d) for q in range(r) for k, l in (("fc1", 0), ("gate_up", 1)) if ROUNDS[q][1] == l
                 for d in range(FT // 2 if l == 0 else FT)] + [(names[0], r, d) for d in range(c)]
            done = [("gelu" if k == "fc1" else "gate", q, d) for k, q, d in o]
            w_ready = LAST_CHUNK["Wfc1"] if layer == 0 else CHUNK_AT[("Wu", 2 * (c // 2))]
            add(key, "PE", 2.6, [("norm_low", "m", 2 * r + 1), ("weight_low", w_ready)] + o[-1:], "hidden", at=a)
            if layer == 0:
                add(("gelu_in", r, c), "ACT", 1.2, [key] + done[-2:-1] + done[-1:][:0], frees=key, at=a)
                add(("gelu_poly", r, c), "Pool", 0.8, [("gelu_in", r, c)] + done[-2:-1]
                    + [("modulate", CHUNK_AT[("tw2", 0)])], at=a)
                add(("gelu_inner", r, c), "DVE", 0.6, [("gelu_poly", r, c)], at=a)
                add(("tanh", r, c), "ACT", 0.5, [("gelu_inner", r, c)] + [("tanh",) + d[1:] for d in o[-1:]], at=a)
                add(("gelu", r, c), "DVE", 0.6, [("tanh", r, c)] + down_before + done[-1:], at=a)
            else:
                add(("tanh", r, c), "ACT", 0.3, [key] + [("tanh",) + d[1:] for d in o[-1:]] + done[-2:-1], at=a)
                add(("gate", r, c), "DVE", 0.85, [("tanh", r, c)] + down_before + done[-1:], frees=key, at=a)
        done = ("gelu" if layer == 0 else "gate", r, chunks - 1)
        for j, n in enumerate(ns):
            a = base + (SLOT - 4) * (0.6 + 0.2 * j)
            add(("down", n), "PE", 3.5, [done, ("weight_low", LAST_CHUNK["Wfc2" if layer == 0 else "Wd"]),
                                        prev(("down",), n)], "linear", at=a)
            add(("residual", "m", n), "DVE", 0.7 if layer == 0 else 0.35, [("down", n), prev(("residual", "m"), n)]
                + ([("gamma_load", pair)] if layer == 0 else [])
                + ([("residual_add", "m", q) for q in (n - 1,) if ("residual_add", "m", q) in steps]),
                frees=("down", n), at=a)
            if layer == 0:
                add(("residual_add", "m", n), "Pool", 0.7, [("residual", "m", n)], at=a)
            else:
                add(("store", n), "SP", 0.5, [("residual", "m", n)] + [("store", q) for q in range(n)
                                                                       if ("store", q) in steps][-1:], at=a)
        last_m0 = ("residual", "m", ns[1])
        if layer == 0:
            for q in range(PAIRS):
                if q == pair:
                    after = [("gamma_store",)]
                    if q >= 2:
                        after += [("residual", "m", 2 * ROUND_OF[(q - 2, 0)] + 1)]
                    if q >= 1:
                        after += [("gamma_load", q - 1)]
                    add(("gamma_load", q), "SP", 1.0, after, at=SLOT * r + START)
    return steps


def make_orders():
    steps = list_steps()
    users = {k: [] for k in steps}
    waiting = {}
    for k, (_, _, after, _, _, _) in steps.items():
        after = set(after)
        waiting[k] = len(after)
        for a in after:
            users[a].append(k)
    ready = {e: [] for e in ("PE", "DVE", "ACT", "Pool", "SP")}
    busy = {e: None for e in ready}
    orders = {e: [] for e in ready}
    free = {kind: list(banks) for kind, banks in BANK_KINDS.items()}
    used = {b: 0 for b in BANKS}
    plan, events, now, left = {}, [], 0.0, len(steps)
    for k, v in steps.items():
        if waiting[k] == 0:
            ready[v[0]].append((v[5], k))
    while left:
        for e in ready:
            if busy[e] is not None:
                continue
            for rank, k in sorted(ready[e], key=lambda v: v[0]):
                fills = steps[k][3]
                if fills and not free[fills]:
                    continue
                if fills:
                    b = free[fills].pop(0)
                    plan[k] = (b, used[b])
                    used[b] += 1
                ready[e].remove((rank, k))
                orders[e].append(k)
                busy[e] = k
                events.append((now + steps[k][1], 0, k))
                break
        if not events:
            raise ValueError("no step can run: " + str([r[:3] for r in ready.values()]))
        events.sort(key=lambda v: v[0])
        now, what, k = events.pop(0)
        if what == 0:
            busy[steps[k][0]] = None
            left -= 1
            events.append((now + WAKE + (2.0 if k[0] in ("load", "gamma_load") else 0.0), 1, k))
        else:
            if steps[k][4]:
                b = plan[steps[k][4]][0]
                free[b.rstrip("01")].append(b)
            for u in users[k]:
                waiting[u] -= 1
                if waiting[u] == 0:
                    ready[steps[u][0]].append((steps[u][5], u))
    return orders, plan, now


ORDER, PLAN, PLANNED_US = make_orders()


def build(nc, x, cond, pos, mask, w, out):
    with ExitStack() as ctx:
        def sb(name, shape, dt=F32):
            return ctx.enter_context(nc.sbuf_tensor(name, shape, dt))

        def sem(name):
            return ctx.enter_context(nc.semaphore(name))

        psum = {b: ctx.enter_context(nc.psum_tensor("ps_" + b, [P, 512], F32)) for b in BANKS}
        filled = {b: sem("filled_" + b) for b in BANKS}
        freed = {b: sem("freed_" + b) for b in BANKS}

        def pair_of(name, shape):
            return sb(name + "_hi", shape, F32R), sb(name + "_lo", shape, F32R)

        WT = {"Wqkv": pair_of("WqkvT", [P, CT, 3 * C]), "Wfc1": pair_of("Wfc1T", [P, CT, HID]),
              "Wqkv1": pair_of("Wqkv1T", [P, CT, QKV1]),
              "Wg": pair_of("WgT", [P, CT, HID]), "Wu": pair_of("WuT", [P, CT, HID])}
        WT1 = {"Wproj": sb("WprojT", [P, CT, C]), "Wo": sb("WoT", [P, CT, C]),
               "Wfc2": sb("Wfc2T", [P, FT, C]), "Wd": sb("WdT", [P, FT, C])}
        stage = sb("stage", [P, STAGE, 4 * P])
        ident = sb("ident", [P, P])
        ident16 = sb("ident16", [P, P], F16)
        minus_half = sb("minus_half", [P, 2 * H0])
        inv_freq = sb("inv_freq", [P, D1 // 2])

        g_u = sb("g_u", [P, 2, 2 * 2 * P])
        g_b = sb("g_b", [P, 2, 2 * 2 * P])
        g_h = sb("g_h", [P, FT, 2 * P])
        adaT = g_b[:, :, :].rearrange("p s (a b) -> p s a b", a=CT)
        cond8, cond_t, silu8 = [g_h[0:N_SEQ, i, :] for i in range(3)]
        bada8 = g_h[0:N_SEQ, 3:5, :].rearrange("p a b -> p (a b)")
        gamma8 = g_h[0:N_SEQ, 5:7, :].rearrange("p a b -> p (a b)")
        vec_rows = g_h[0:12 + FT + 2 * CT, 7, 0:P]
        red = g_u[:, :, :].rearrange("p a b -> p (a b)")[:, 0:3 * 2 * N_SEQ * D1 // 2].rearrange(
            "p (a b c d) -> p a b c d", a=3, b=2, c=N_SEQ)
        ang = g_u[:, :, :].rearrange("p a b -> p (a b)")[:, 3 * 2 * N_SEQ * D1 // 2:7 * N_SEQ * D1 // 2].rearrange(
            "p (c d) -> p c d", c=N_SEQ)

        N_VEC = 12 + FT + 2 * CT
        cols = sb("cols", [P, 4 * N_SEQ + N_VEC])
        V0 = 4 * N_SEQ
        V_BADA, V_BFC1, V_LN1, V_LN2 = V0, V0 + 12, V0 + 12 + FT, V0 + 12 + FT + CT
        modul = sb("modul", [P, 6, CT, N_SEQ])
        gamma_dram = nc.dram_tensor("gamma_scratch", (N_SEQ, 2 * C), F32).ap()
        gamma = sb("gamma", [P, 2, 2, 2 * C])
        qk_bias = sb("qk_bias", [P, 2 * C])
        v_bias = sb("v_bias", [P, C])
        res_bias = sb("res_bias", [P, 2, C])
        head_scale = sb("head_scale", [P, H0])
        head_log = sb("head_log", [P, H0])
        bias_mask = sb("bias_mask", [P, P])
        pos_i = sb("pos_i", [P, N_SEQ], I32)
        pos_f = sb("pos_f", [P, N_SEQ])
        HALF = D1 // 2
        turns = sb("turns", [P, 2, N_SEQ, HALF])
        cos_t = sb("cos_t", [P, N_SEQ, HALF])
        sin_t = sb("sin_t", [P, N_SEQ, 2, HALF])

        X = sb("X", [P, N_SEQ, C])
        stats = sb("stats", [P, 32, 6])
        mean_var = sb("mean_var", [P, 32, 2])
        msq = sb("msq", [P, 32, 2])
        rstd = sb("rstd", [P, 32, 1])
        NM = {"a": 0, "m": 1}
        xn = sb("xn", [P, 2, 2, C])
        h_full = xn[:, :, :, :].rearrange("p m j (c t) -> p m j c t", t=P)
        h_hi = sb("h_hi", [P, 2, CT, 2 * P], F32R)
        h_lo = sb("h_lo", [P, 2, CT, 2 * P], F32R)
        qk = sb("qk", [P, 2, 2 * C])
        qk_ss = sb("qk_ss", [P, 2, 2 * H0])
        qk_fl = sb("qk_fl", [P, 2, 2 * H0])
        qk_r = sb("qk_r", [P, 2, 2 * H0])
        qk_rs = sb("qk_rs", [P, 2, 2 * H0])
        qk_n = sb("qk_n", [P, 2, 2 * C])
        qk_sq = qk_n
        qk_pack = sb("qk_pack", [P, 2, 3, H0, QUAD], F16)
        qkT = sb("qkT", [P, 2, 3, 4, P], F16)
        v_pad = sb("v_pad", [P, 2, H0, QUAD])
        qkv1 = sb("qkv1", [P, 2, QKV1])
        rope_c = sb("rope_c", [P, 9, 2, HALF])
        rope_s = sb("rope_s", [P, 9, 2, HALF])
        qk1_rot = sb("qk1_rot", [P, 2, 12, D1])
        qk1T = sb("qk1T", [P, 2, 3, P])
        z = sb("z", [P, 2, 4, P])
        row_sum = sb("row_sum", [P, 2, 4])
        row_inv = sb("row_inv", [P, 2, 4])
        neg_max = sb("neg_max", [P, 2, 4])
        neg_max_s = sb("neg_max_s", [P, 2, 4])
        probs = z
        probsT = sb("probsT", [P, 2, 4, P])
        o_full = sb("o_full", [P, 2, CT, P])
        res_t = sb("res_t", [P, 2, 2, C])
        g_a = sb("g_a", [P, 2, 2 * 2 * P])

        stage_loaded = [sem(f"stage_loaded{i}") for i in range(STAGE)]
        small_loaded = sem("small_loaded")
        vec_loaded = sem("vec_loaded")
        x_loaded = [sem(f"x_loaded{i}") for i in range(PAIRS)]
        gamma_stored, out_stored = sem("gamma_stored"), sem("out_stored")
        gamma_loaded = [sem(f"gamma_loaded{i}") for i in range(PAIRS)]
        consts_set, zeroed = sem("consts_set"), sem("zeroed")
        cond_tanh, cond_silu, silu_mid = sem("cond_tanh"), sem("cond_silu"), sem("silu_mid")
        weight_high = sem("weight_high")
        table_step, angles_ready, table_ready = sem("table_step"), sem("angles_ready"), sem("table_ready")
        scale_clipped, scale_ready = sem("scale_clipped"), sem("scale_ready")

        def both(name):
            return {k: sem(f"{name}_{k}") for k in "am"}

        stats_mid, stats_aggr, stats_ready, rstd_mid, rstd_ready = (both("stats_mid"), both("stats_aggr"),
                                                                    both("stats_ready"), both("rstd_mid"),
                                                                    both("rstd_ready"))
        xn_ready, h_high, h_low = both("xn_ready"), both("h_high"), both("h_low")
        qk_squared, qk_summed, qk_floor = sem("qk_squared"), sem("qk_summed"), sem("qk_floor")
        qk_root, qk_rnorm, qk_normed = sem("qk_root"), sem("qk_rnorm"), sem("qk_normed")
        qk_high, qk_low, qk_packed = sem("qk_high"), sem("qk_low"), sem("qk_packed")
        rope_parts, rope_ready = sem("rope_parts"), sem("rope_ready")
        max_raw, max_ready, exp_ready, inv_ready, probs_ready = (sem("max_raw"), sem("max_ready"), sem("exp_ready"),
                                                                 sem("inv_ready"), sem("probs_ready"))
        values_summed = sem("values_summed")
        res_scaled, res_ready = both("res_scaled"), both("res_ready")
        g_squared, g_poly, g_inner, g_tanh, g_gated, g_ready = [
            sem(n) for n in ("g_squared", "g_poly", "g_inner", "g_tanh", "g_gated", "g_ready")]

        def is_filled(key):
            b, t = PLAN[key]
            return filled[b], t + 1

        def is_freed(key):
            b, t = PLAN[key]
            return freed[b], t + 1

        def bank_of(key):
            return psum[PLAN[key][0]]

        def last_product(kind, r):
            if kind == "m":
                return ("fc1", r, FT // 2 - 1) if ROUNDS[r][1] == 0 else ("gate_up", r, FT - 1)
            return ("v_product", 2 * r + 1) if ROUNDS[r][1] == 0 else ("qkv1_product", 2 * r + 1)

        def mlp_ord(r, c):
            return sum((FT // 2 if ROUNDS[q][1] == 0 else FT) for q in range(r)) + c

        def ord0(n):
            return 2 * sum(1 for q in range(n // 2) if ROUNDS[q][1] == 0) + n % 2

        def ord1(n):
            return 2 * sum(1 for q in range(n // 2) if ROUNDS[q][1] == 1) + n % 2

        def splits_before(c):
            return sum(1 for q in range(c) if q not in IS_ADA and CHUNKS[q][0] not in WT1)

        def gu_ord(r, f):
            return sum(1 for q in range(r) if ROUNDS[q][1] == 1) * FT + f

        def at_ord1(o):
            return [n for n in range(2 * len(ROUNDS)) if layer_of(n) == 1][o]

        def fc_ord(r, c):
            return sum(1 for q in range(r) if ROUNDS[q][1] == 0) * (FT // 2) + c

        def at_ord0(o):
            return [n for n in range(2 * len(ROUNDS)) if layer_of(n) == 0][o]

        def ada_chunk(o):
            return [c for c in IS_ADA if IS_ADA[c] == o][0]

        def ready_before(kind, n):
            pair, layer = ROUNDS[n // 2]
            if kind == "m":
                return is_freed(("project", n)) if layer == 1 else (res_ready["a"], ord0(n) + 1)
            if layer == 0:
                return x_loaded[pair], 16
            return res_ready["m"], ord0(2 * ROUND_OF[(pair, 0)] + n % 2) + 1

        def weight_views(c, bank):
            name, i = CHUNKS[c]
            src = bank[:, :].rearrange("p (a b) -> p a b", b=256)
            if name in WIDE:
                hi, lo = WT1[name], WT1[name]
                r, c0 = i // 2, 4 * (i % 2)
                sl = (slice(None), slice(c0, c0 + 4), slice(r * P, (r + 1) * P))
                return hi[sl], lo[sl], bank[:, :].rearrange("p (a b) -> p a b", b=P)
            if name == "Wkv":
                hi, lo = WT["Wqkv1"]
                sl = (slice(None), slice(None), slice(C, QKV1))
                return hi[sl], lo[sl], bank[:, 0:4 * D1].rearrange("p (a b) -> p a b", b=2 * D1)
            if name == "Wq":
                hi, lo = WT["Wqkv1"]
                sl = (slice(None), slice(None), slice(0, C))
                return hi[sl], lo[sl], src
            hi, lo = WT[name] if name in WT else (WT1[name], WT1[name])
            sl = (slice(None), slice(None), slice(i * P, (i + 2) * P))
            return hi[sl], lo[sl], src

        N_SMALL = 9
        block = ctx.enter_context(nc.Block())

        @block.sync
        def _(sp):
            def bcast(v, rows):
                return v.partition_broadcast(rows)

            def load(c):
                name, i = CHUNKS[c]
                done = stage_loaded[c % STAGE]
                if c >= STAGE:
                    sp.wait_ge(*is_filled(("weight_turn", c - STAGE)))
                dst = stage[:, c % STAGE, :]
                if name == "Wkv":
                    sp.dma_start(dst[0:D1, 0:C], w["Wk"]).then_inc(done, 16)
                    sp.dma_start(dst[D1:2 * D1, 0:C], w["Wv"]).then_inc(done, 16)
                elif name in WIDE:
                    src = w[name][(i // 2) * P:(i // 2 + 1) * P, (i % 2) * 512:(i % 2 + 1) * 512]
                    sp.dma_start(dst, src).then_inc(done, 16)
                else:
                    row = i * C if name == "ada" else i * P
                    src = w["Wada" if name == "ada" else name][row:row + 2 * P, :]
                    sp.dma_start(dst.rearrange("p (t i) -> p t i", t=2),
                                 src.rearrange("(t p) i -> p t i", p=P)).then_inc(done, 16)

            def load_x(p):
                sp.dma_start(X[:, 2 * p:2 * p + 2, :],
                             x[2 * p:2 * p + 2].rearrange("n t c -> t n c")).then_inc(x_loaded[p], 16)

            def gamma_store():
                sp.wait_ge(*is_freed(("modulate", CHUNK_AT[("ada", ADA["gamma2"])])))
                sp.dma_start(gamma_dram, gamma8[:, :]).then_inc(gamma_stored, 16)
                sp.wait_ge(gamma_stored, 16)

            def gamma_load(p):
                if p >= 2:
                    sp.wait_ge(res_scaled["m"], ord0(2 * ROUND_OF[(p - 2, 0)] + 1) + 1)
                for j in range(2):
                    sp.dma_start(gamma[:, p % 2, j, :],
                                 gamma_dram[2 * p + j].partition_broadcast(P)).then_inc(gamma_loaded[p], 16)

            def store(n):
                sp.wait_ge(*is_freed(("down", n)))
                sp.dma_start(out[seq_of(n)], X[:, seq_of(n), :]).then_inc(out_stored, 16)

            sp.dma_start(cond8[:, :], cond).then_inc(vec_loaded, 16)
            sp.dma_start(vec_rows[0:12, :], w["bada"].rearrange("(r p) -> r p", p=P)).then_inc(vec_loaded, 16)
            sp.dma_start(vec_rows[12:12 + FT, :], w["bfc1"].rearrange("(r p) -> r p", p=P)).then_inc(vec_loaded, 16)
            sp.dma_start(vec_rows[20:22, :], w["ln1_w"].rearrange("(r p) -> r p", p=P)).then_inc(vec_loaded, 16)
            sp.dma_start(vec_rows[22:24, :], w["ln2_w"].rearrange("(r p) -> r p", p=P)).then_inc(vec_loaded, 16)
            for name, *a in ORDER["SP"]:
                {"load": load, "gamma_store": gamma_store, "gamma_load": gamma_load, "store": store}[name](*a)
                if name == "load" and a[0] < PAIRS:
                    load_x(a[0])
                if name == "load" and a[0] == 1:
                    for dst, src in ((pos_i[:, :], pos), (head_log[:, :], bcast(w["sml"], P)),
                                     (qk_bias[:, 0:C], bcast(w["q_bias"], P)), (v_bias[:, :], bcast(w["v_bias"], P)),
                                     (res_bias[:, 0, :], bcast(w["bproj"], P)),
                                     (res_bias[:, 1, :], bcast(w["bfc2"], P)),
                                     (bias_mask[:, :], mask), (bada8[:, 0:C], bcast(w["bada"][0:C], N_SEQ)),
                                     (bada8[:, C:2 * C], bcast(w["bada"][C:2 * C], N_SEQ))):
                        sp.dma_start(dst, src).then_inc(small_loaded, 16)
            sp.wait_ge(out_stored, 16 * N_SEQ)

        @block.gpsimd
        def _(pool):
            pool.memset(ident[:, :], 0.0).then_inc(zeroed, 1)
            pool.wait_ge(zeroed, 1)
            pool.affine_select(out=ident[:, :], in_=ident[:, :], compare_op=ALU.not_equal, fill=1.0, base=0,
                               pattern=[[-1, P]], channel_multiplier=1).then_inc(consts_set, 1)
            pool.memset(minus_half[:, :], -0.5)
            pool.memset(v_pad[:, :, :, :], 0.0)
            pool.memset(qk_bias[:, C:2 * C], 0.0)
            for f in range(HALF):
                pool.memset(inv_freq[:, f:f + 1], float(np.float32(1.0) / np.float32(
                    np.float32(10000.0) ** np.float32(2.0 * f / D1))))
            pool.wait_ge(consts_set, 1)
            pool.tensor_copy(ident16[:, :], ident[:, :]).then_inc(consts_set, 1)

            def norm_root(kind, n):
                k = NM[kind] * 16 + n
                pool.wait_ge(stats_ready[kind], n + 1)
                pool.tensor_scalar(msq[:, k, 1:2], msq[:, k, 0:1], LN_EPS, None, ALU.add).then_inc(rstd_mid[kind], 1)
                pool.wait_ge(rstd_mid[kind], n + 1)
                pool.tensor_tensor(rstd[:, k, :], msq[:, k, 1:2], minus_half[:, 0:1],
                                   ALU.pow).then_inc(rstd_ready[kind], 1)

            def norm_low(kind, n):
                m, j = NM[kind], n % 2
                pool.wait_ge(h_high[kind], n + 1)
                pool.tensor_tensor(h_lo[:, m, :, j * P:(j + 1) * P], h_full[:, m, j, :, :],
                                   h_hi[:, m, :, j * P:(j + 1) * P].bitcast(F32),
                                   ALU.subtract).then_inc(h_low[kind], 1)

            def qk_root_(n):
                o, j = ord0(n), n % 2
                pool.wait_ge(qk_floor, o + 1)
                pool.tensor_tensor(qk_r[:, j, :], qk_fl[:, j, :], minus_half[:, :], ALU.pow).then_inc(qk_root, 1)
                pool.wait_ge(qk_root, o + 1)
                if o == 0:
                    pool.wait_ge(scale_ready, 1)
                if o >= 2:
                    pool.wait_ge(qk_normed, o - 1)
                pool.tensor_tensor(qk_rs[:, j, 0:H0], qk_r[:, j, 0:H0], head_scale[:, :], ALU.mult)
                pool.tensor_copy(qk_rs[:, j, H0:2 * H0], qk_r[:, j, H0:2 * H0]).then_inc(qk_rnorm, 1)

            def qk_swap(n):
                o, j = ord0(n), n % 2
                pool.wait_ge(qk_low, o + 1)
                pool.tensor_copy(qk_pack[:, j, 2, :, 0:D0], qk_pack[:, j, 0, :, D0:2 * D0])
                pool.tensor_copy(qk_pack[:, j, 2, :, D0:2 * D0], qk_pack[:, j, 0, :, 0:D0]).then_inc(qk_packed, 1)

            def norm_probs(G):
                U = len(heads_of(G))
                pool.wait_ge(inv_ready, G + 1)
                pool.tensor_tensor(z[:, G % 2, 0:U, :], z[:, G % 2, 0:U, :],
                                   row_inv[:, G % 2, 0:U].unsqueeze(2).to_broadcast([P, U, P]),
                                   ALU.mult).then_inc(probs_ready, 1)

            def residual_add(kind, n):
                pool.wait_ge(res_scaled[kind], ord0(n) + 1)
                s = seq_of(n)
                pool.tensor_tensor(X[:, s, :], X[:, s, :], res_t[:, NM[kind], 1, :],
                                   ALU.add).then_inc(res_ready[kind], 1)

            def gelu_poly(r, c):
                o = fc_ord(r, c)
                pool.wait_ge(g_squared, o + 1)
                if o >= 2:
                    pool.wait_ge(g_inner, o - 1)
                else:
                    pool.wait_ge(*is_filled(("modulate", ada_chunk(len(IS_ADA) - 1))))
                pool.tensor_scalar(g_b[:, o % 2, :], g_a[:, o % 2, :], 0.044715, 1.0, ALU.mult,
                                   ALU.add).then_inc(g_poly, 1)

            steps = {"norm_root": norm_root, "norm_low": norm_low, "qk_root": qk_root_, "qk_swap": qk_swap,
                     "norm_probs": norm_probs, "residual_add": residual_add, "gelu_poly": gelu_poly}
            for name, *a in ORDER["Pool"]:
                steps[name](*a)

        @block.scalar
        def _(act):
            def cond_tanh_():
                act.wait_ge(vec_loaded, 16 * 5)
                act.activation(cond_t[:, :], cond8[:, :], ACT.Tanh, scale=0.5).then_inc(cond_tanh, 1)

            def sines():
                act.wait_ge(angles_ready, 1)
                act.activation(sin_t[:, :, 0, :], red[:, 2, 1, :, :], ACT.Sin, scale=-1.0)
                act.activation(sin_t[:, :, 1, :], red[:, 2, 1, :, :], ACT.Sin)
                act.activation(cos_t[:, :, :], red[:, 2, 0, :, :], ACT.Sin).then_inc(table_ready, 1)
                act.wait_ge(scale_clipped, 1)
                act.activation(head_scale[:, :], head_log[:, :], ACT.Exp).then_inc(scale_ready, 1)

            def weight_high_(c):
                act.wait_ge(*is_filled(("weight_turn", c)))
                hi, _, src = weight_views(c, bank_of(("weight_turn", c)))
                act.activation(hi, src, ACT.Copy).then_inc(weight_high, 1)

            def norm_high(kind, n):
                m, j = NM[kind], n % 2
                act.wait_ge(*is_freed(("norm_turn", kind, n)))
                if n >= 2:
                    act.wait_ge(*is_filled(last_product(kind, n // 2 - 1)))
                act.activation(h_hi[:, m, :, j * P:(j + 1) * P], h_full[:, m, j, :, :],
                               ACT.Copy).then_inc(h_high[kind], 1)

            def qk_square(n):
                o, j = ord0(n), n % 2
                act.wait_ge(*is_freed(("qk_product", n)))
                if o >= 2:
                    act.wait_ge(qk_low, o - 1)
                act.activation(qk_sq[:, j, :], qk[:, j, :], ACT.Square).then_inc(qk_squared, 1)

            def qk_high_(n):
                o, j = ord0(n), n % 2
                act.wait_ge(qk_normed, o + 1)
                if o >= 2:
                    act.wait_ge(*is_filled(("k_turn", at_ord0(o - 2))))
                act.activation(qk_pack[:, j, 0:2, :, 0:D0],
                               qk_n[:, j, :].rearrange("p (s h d) -> p s h d", s=2, d=D0),
                               ACT.Copy).then_inc(qk_high, 1)

            def qkv1_copy(n):
                o, j = ord1(n), n % 2
                key = ("qkv1_product", n)
                act.wait_ge(*is_filled(key))
                if o >= 2:
                    act.wait_ge(rope_ready, o - 1)
                if n >= 2:
                    act.wait_ge(values_summed, 4 * (n - 1))
                act.activation(qkv1[:, j, :], bank_of(key)[:, 0:QKV1], ACT.Copy).then_inc(is_freed(key)[0], 1)

            def exp(G):
                n, heads = G // 4, heads_of(G)
                key = ("scores", G)
                act.wait_ge(max_ready, G + 1)
                for u in range(len(heads)):
                    total = row_sum[:, G % 2, u:u + 1]
                    if layer_of(n) == 0:
                        ins = act.activation(z[:, G % 2, u, :], z[:, G % 2, u, :], ACT.Exp,
                                             bias=neg_max[:, G % 2, u:u + 1], accum_out=total)
                    else:
                        ins = act.activation(z[:, G % 2, u, :], bank_of(key)[:, u * P:(u + 1) * P], ACT.Exp,
                                             bias=neg_max_s[:, G % 2, u:u + 1], scale=SCORE_SCALE1, accum_out=total)
                ins.then_inc(exp_ready, 1)

            def probs_copy(G):
                key, U = ("probs_turn", G), len(heads_of(G))
                act.wait_ge(*is_filled(key))
                if G >= 2:
                    act.wait_ge(values_summed, G - 1)
                act.activation(probsT[:, G % 2, 0:U, :], bank_of(key)[:, 0:U * P].rearrange("p (u q) -> p u q", u=U),
                               ACT.Copy).then_inc(is_freed(key)[0], 1)

            def attn_copy(n):
                key = ("values", 4 * n)
                act.wait_ge(values_summed, 4 * n + 4)
                if n >= 2:
                    act.wait_ge(*is_filled(("project", n - 2)))
                act.activation(o_full[:, n % 2, :, :], bank_of(key)[:, 0:C].rearrange("p (c q) -> p c q", c=CT),
                               ACT.Copy).then_inc(is_freed(key)[0], 1)

            def gelu_in(r, c):
                o, key = fc_ord(r, c), ("fc1", r, c)
                act.wait_ge(*is_filled(key))
                if mlp_ord(r, c) >= 2:
                    act.wait_ge(g_ready, mlp_ord(r, c) - 1)
                for s in range(2):
                    f = 2 * c + s
                    ins = act.activation(g_u[:, o % 2, s * 256:(s + 1) * 256],
                                         bank_of(key)[:, s * 256:(s + 1) * 256],
                                         ACT.Identity, bias=cols[:, V_BFC1 + f:V_BFC1 + f + 1])
                ins.then_inc(is_freed(key)[0], 1)
                act.wait_ge(*is_freed(key))
                act.activation(g_a[:, o % 2, :], g_u[:, o % 2, :], ACT.Square).then_inc(g_squared, 1)

            def tanh(r, c):
                m = mlp_ord(r, c)
                if ROUNDS[r][1] == 0:
                    o = fc_ord(r, c)
                    act.wait_ge(g_inner, o + 1)
                    act.activation(g_a[:, o % 2, :], g_a[:, o % 2, :], ACT.Tanh, scale=GELU_C).then_inc(g_tanh, 1)
                    return
                key = ("gate_up", r, c)
                act.wait_ge(*is_filled(key))
                act.wait_ge(g_ready, m - 1)
                act.activation(g_a[:, c % 2, 0:256], bank_of(key)[:, 0:256], ACT.Tanh, scale=0.5).then_inc(g_tanh, 1)

            steps = {"cond_tanh": cond_tanh_, "sines": sines, "weight_high": weight_high_, "norm_high": norm_high,
                     "qk_square": qk_square, "qk_high": qk_high_, "qkv1_copy": qkv1_copy, "exp": exp,
                     "probs_copy": probs_copy, "attn_copy": attn_copy, "gelu_in": gelu_in, "tanh": tanh}
            for name, *a in ORDER["ACT"]:
                steps[name](*a)

        @block.vector
        def _(dve):
            def cond_silu_():
                dve.wait_ge(cond_tanh, 1)
                dve.scalar_tensor_tensor(out=cond_t[:, :], in0=cond_t[:, :], scalar=1.0, in1=cond8[:, :],
                                         op0=ALU.add, op1=ALU.mult).then_inc(silu_mid, 1)
                dve.wait_ge(silu_mid, 1)
                dve.tensor_scalar(silu8[:, :], cond_t[:, :], 0.5, None, ALU.mult).then_inc(cond_silu, 1)

            def cond_copy():
                key = ("cond_turn",)
                dve.wait_ge(*is_filled(key))
                dve.tensor_copy(cols[:, :], bank_of(key)[:, 0:V0 + N_VEC]).then_inc(is_freed(key)[0], 1)

            tick = [0]

            def link(ins):
                ins.then_inc(table_step, 1)
                tick[0] += 1
                dve.wait_ge(table_step, tick[0])

            def angles():
                dve.wait_ge(small_loaded, 16 * N_SMALL)
                dve.tensor_scalar(head_log[:, :], head_log[:, :], MAX_LOG_SCALE, None,
                                  ALU.min).then_inc(scale_clipped, 1)
                dve.wait_ge(consts_set, 2)
                link(dve.tensor_copy(pos_f[:, :], pos_i[:, :]))
                link(dve.tensor_tensor(ang, pos_f[:, :].unsqueeze(2).to_broadcast([P, N_SEQ, HALF]),
                                       inv_freq[:, :].unsqueeze(1).to_broadcast([P, N_SEQ, HALF]), ALU.mult))
                dve.tensor_scalar(red[:, 0, 0, :, :], ang, 1.0 / TWO_PI, 0.25, ALU.mult, ALU.add)
                link(dve.tensor_scalar(red[:, 0, 1, :, :], ang, 1.0 / TWO_PI, None, ALU.mult))
                link(dve.tensor_scalar(turns[:, :, :, :], red[:, 0, :, :, :], ROUND_MAGIC, ROUND_MAGIC, ALU.add,
                                       ALU.subtract))
                a2 = ang.rearrange("p n f -> p (n f)").unsqueeze(1).to_broadcast([P, 2, N_SEQ * HALF])
                fl = [red[:, i, :, :, :].rearrange("p s n f -> p s (n f)") for i in range(3)]
                tf = turns[:, :, :, :].rearrange("p s n f -> p s (n f)")
                link(dve.scalar_tensor_tensor(out=fl[0], in0=tf, scalar=-PI_1, in1=a2, op0=ALU.mult, op1=ALU.add))
                link(dve.scalar_tensor_tensor(out=fl[1], in0=tf, scalar=-PI_2, in1=fl[0], op0=ALU.mult,
                                              op1=ALU.add))
                link(dve.scalar_tensor_tensor(out=fl[0], in0=tf, scalar=-PI_3, in1=fl[1], op0=ALU.mult,
                                              op1=ALU.add))
                dve.tensor_copy(red[:, 1, 1, :, :], red[:, 0, 1, :, :])
                link(dve.tensor_scalar(red[:, 1, 0, :, :], red[:, 0, 0, :, :], float(np.pi / 2), None, ALU.add))
                dve.tensor_scalar(red[:, 2, :, :, :], red[:, 1, :, :, :], SIN_LIMIT, -SIN_LIMIT, ALU.min,
                                  ALU.max).then_inc(angles_ready, 1)

            def weight_low(c):
                key = ("weight_turn", c)
                hi, lo, src = (None,) * 3
                if c in IS_ADA:
                    o = IS_ADA[c]
                    dve.wait_ge(*is_filled(key))
                    if o >= 2:
                        dve.wait_ge(*is_filled(("modulate", ada_chunk(o - 2))))
                    ins = dve.tensor_copy(adaT[:, o % 2, :, :], bank_of(key)[:, :].rearrange("p (a b) -> p a b", b=C))
                elif CHUNKS[c][0] in WHOLE:
                    hi, _, src = weight_views(c, bank_of(key))
                    dve.wait_ge(*is_filled(key))
                    ins = dve.tensor_scalar(hi, src, 0.5 if CHUNKS[c][0] == "Wfc2" else 1.0, None, ALU.mult)
                else:
                    hi, lo, src = weight_views(c, bank_of(key))
                    dve.wait_ge(weight_high, splits_before(c) + 1)
                    ins = dve.tensor_tensor(lo, src, hi.bitcast(F32), ALU.subtract)
                ins.then_inc(is_freed(key)[0], 1)

            def modulated(c):
                key, bank, chunk = ("modulate", c), bank_of(("modulate", c)), CHUNKS[c]
                dve.wait_ge(*is_filled(key))
                if chunk[0] == "ada" and chunk[1] < 2:
                    g = chunk[1]
                    dve.wait_ge(small_loaded, 16 * N_SMALL)
                    ins = dve.tensor_tensor(gamma8[:, g * C:(g + 1) * C], bank[0:N_SEQ, 0:C],
                                            bada8[:, g * C:(g + 1) * C], ALU.add)
                else:
                    m = MOD_OF[chunk]
                    for ft in range(CT):
                        src, dst = bank[:, ft * N_SEQ:(ft + 1) * N_SEQ], modul[:, m, ft, :]
                        if chunk[0] == "ada":
                            v = V_BADA + CT * chunk[1] + ft
                            is_scale = chunk[1] in (ADA["scale1"], ADA["scale2"])
                            ins = dve.tensor_scalar(dst, src, cols[:, v:v + 1], 1.0 if is_scale else 0.0,
                                                    ALU.add, ALU.add)
                        else:
                            v = (V_LN1 if chunk[0] == "tw1" else V_LN2) + ft
                            ins = dve.tensor_scalar(dst, src, 1.0, cols[:, v:v + 1], ALU.add, ALU.mult)
                ins.then_inc(is_freed(key)[0], 1)

            def norm_stats(kind, n):
                k, s = NM[kind] * 16 + n, seq_of(n)
                dve.wait_ge(*ready_before(kind, n))
                dve.bn_stats(stats[:, k, :], X[:, s, :]).then_inc(stats_mid[kind], 1)
                dve.wait_ge(stats_mid[kind], n + 1)
                if layer_of(n) == 0:
                    dve.bn_aggr(mean_var[:, k, :], stats[:, k, :]).then_inc(stats_aggr[kind], 1)
                    dve.wait_ge(stats_aggr[kind], n + 1)
                    dve.tensor_copy(msq[:, k, 0:1], mean_var[:, k, 1:2]).then_inc(stats_ready[kind], 1)
                else:
                    dve.bn_aggr(mean_var[:, k, :], stats[:, k, :]).then_inc(stats_aggr[kind], 1)
                    dve.wait_ge(stats_aggr[kind], n + 1)
                    dve.scalar_tensor_tensor(out=msq[:, k, 0:1], in0=mean_var[:, k, 0:1],
                                             scalar=mean_var[:, k, 0:1], in1=mean_var[:, k, 1:2],
                                             op0=ALU.mult, op1=ALU.add).then_inc(stats_ready[kind], 1)

            def norm_apply(kind, n):
                m, k, s = NM[kind], NM[kind] * 16 + n, seq_of(n)
                dve.wait_ge(rstd_ready[kind], n + 1)
                if n >= 2:
                    dve.wait_ge(h_low[kind], n - 1)
                if layer_of(n) == 0:
                    dve.tensor_scalar(xn[:, m, n % 2, :], X[:, s, :], mean_var[:, k, 0:1], rstd[:, k, :],
                                      ALU.subtract, ALU.mult).then_inc(xn_ready[kind], 1)
                else:
                    dve.tensor_scalar(xn[:, m, n % 2, :], X[:, s, :], rstd[:, k, :], None,
                                      ALU.mult).then_inc(xn_ready[kind], 1)

            def norm_mod(kind, n):
                m, j, s = NM[kind], n % 2, seq_of(n)
                key = ("norm_turn", kind, n)
                dve.wait_ge(*is_filled(key))
                for ft in range(CT):
                    src, dst = bank_of(key)[:, ft * P:(ft + 1) * P], h_full[:, m, j, ft, :]
                    if layer_of(n) == 0:
                        k = 0 if kind == "a" else 2
                        ins = dve.tensor_scalar(dst, src, modul[:, k, ft, s:s + 1], modul[:, k + 1, ft, s:s + 1],
                                                ALU.mult, ALU.add)
                    else:
                        k = 4 if kind == "a" else 5
                        ins = dve.tensor_scalar(dst, src, modul[:, k, ft, s:s + 1], None, ALU.mult)
                ins.then_inc(is_freed(key)[0], 1)

            def qk_copy(n):
                o, j, key = ord0(n), n % 2, ("qk_product", n)
                dve.wait_ge(*is_filled(key))
                if o == 0:
                    dve.wait_ge(small_loaded, 16 * N_SMALL)
                    dve.wait_ge(consts_set, 2)
                if o >= 2:
                    dve.wait_ge(qk_normed, o - 1)
                dve.tensor_tensor(qk[:, j, :], bank_of(key)[:, :], qk_bias[:, :], ALU.add
                                  ).then_inc(is_freed(key)[0], 1)

            def v_copy(n):
                j, key = n % 2, ("v_product", n)
                dve.wait_ge(*is_filled(key))
                if n >= 2:
                    dve.wait_ge(values_summed, 4 * (n - 1))
                pv = bank_of(key)[:, 0:C].rearrange("p (h e d) -> p h e d", e=2, d=D0)
                bv = v_bias[:, :].rearrange("p (h e d) -> p h e d", e=2, d=D0)
                dst = v_pad[:, j, :, :].rearrange("p (h e) w -> p h e w", e=2)
                for e in range(2):
                    ins = dve.tensor_tensor(dst[:, :, e, e * D0:(e + 1) * D0], pv[:, :, e, :], bv[:, :, e, :],
                                            ALU.add)
                ins.then_inc(is_freed(key)[0], 1)

            def qk_sum(n):
                o, j = ord0(n), n % 2
                dve.wait_ge(qk_squared, o + 1)
                dve.tensor_reduce(qk_ss[:, j, :], qk_sq[:, j, :].rearrange("p (h d) -> p h d", d=D0), AX_X,
                                  ALU.add).then_inc(qk_summed, 1)
                dve.wait_ge(qk_summed, o + 1)
                dve.tensor_scalar(qk_fl[:, j, :], qk_ss[:, j, :], NORM_FLOOR, None, ALU.max).then_inc(qk_floor, 1)

            def qk_scale(n):
                o, j = ord0(n), n % 2
                dve.wait_ge(qk_rnorm, o + 1)
                v3 = [t[:, j, :].rearrange("p (h d) -> p h d", d=D0) for t in (qk_n, qk)]
                dve.tensor_tensor(v3[0], v3[1], qk_rs[:, j, :].unsqueeze(2).to_broadcast([P, 2 * H0, D0]),
                                  ALU.mult).then_inc(qk_normed, 1)

            def qk_low_(n):
                o, j = ord0(n), n % 2
                dve.wait_ge(qk_high, o + 1)
                for s in range(2):
                    ins = dve.tensor_tensor(qk_pack[:, j, s, :, D0:2 * D0],
                                            qk_n[:, j, s * C:(s + 1) * C].rearrange("p (h d) -> p h d", d=D0),
                                            qk_pack[:, j, s, :, 0:D0], ALU.subtract)
                ins.then_inc(qk_low, 1)

            def q_copy(n):
                j, key = n % 2, ("q_turn", n)
                if n >= 2:
                    dve.wait_ge(exp_ready, 4 * (n - 1))
                dve.wait_ge(*is_filled(key))
                v = bank_of(key)[:, :].bitcast(F16)
                dve.tensor_copy(qkT[:, j, 0, :, :], v[:, 0:512].rearrange("p (g t) -> p g t", g=4))
                dve.tensor_copy(qkT[:, j, 2, :, :], v[:, 512:1024].rearrange("p (g t) -> p g t", g=4)
                                ).then_inc(is_freed(key)[0], 1)

            def k_copy(n):
                j, key = n % 2, ("k_turn", n)
                dve.wait_ge(*is_filled(key))
                v = bank_of(key)[:, :].bitcast(F16)
                dve.tensor_copy(qkT[:, j, 1, :, :], v[:, 0:512].rearrange("p (g t) -> p g t", g=4)
                                ).then_inc(is_freed(key)[0], 1)

            def rope(n):
                o, j, s = ord1(n), n % 2, seq_of(n)
                dve.wait_ge(*is_freed(("qkv1_product", n)))
                if o == 0:
                    dve.wait_ge(table_ready, 1)
                if o >= 1:
                    dve.wait_ge(rope_ready, o)
                src = qkv1[:, j, 0:C + D1].rearrange("p (h e f) -> p h e f", e=2, f=HALF)
                cs = cos_t[:, s, :].unsqueeze(1).to_broadcast([P, 18, HALF])
                dve.tensor_tensor(rope_c[:, :, :, :].rearrange("p h e f -> p (h e) f"),
                                  qkv1[:, j, 0:C + D1].rearrange("p (h f) -> p h f", f=HALF), cs, ALU.mult)
                for e in range(2):
                    sn = sin_t[:, s, e, :].unsqueeze(1).to_broadcast([P, 9, HALF])
                    ins = dve.tensor_tensor(rope_s[:, :, e, :], src[:, :, 1 - e, :], sn, ALU.mult)
                ins.then_inc(rope_parts, 1)
                dve.wait_ge(rope_parts, o + 1)
                if o >= 2:
                    dve.wait_ge(*is_filled(("qk1_turn", at_ord1(o - 2))))
                rc = rope_c[:, :, :, :].rearrange("p h e f -> p h (e f)")
                rs = rope_s[:, :, :, :].rearrange("p h e f -> p h (e f)")
                dve.tensor_tensor(qk1_rot[:, j, 0:H1, :], rc[:, 0:H1, :], rs[:, 0:H1, :], ALU.add)
                dve.tensor_tensor(qk1_rot[:, j, H1:H1 + 4, :], rc[:, H1:H1 + 1, :].to_broadcast([P, 4, D1]),
                                  rs[:, H1:H1 + 1, :].to_broadcast([P, 4, D1]), ALU.add).then_inc(rope_ready, 1)

            def qk1_copy(n):
                j, key = n % 2, ("qk1_turn", n)
                if n >= 2:
                    dve.wait_ge(exp_ready, 4 * (n - 1))
                dve.wait_ge(*is_filled(key))
                dve.tensor_copy(qk1T[:, j, :, :], bank_of(key)[:, 0:3 * P].rearrange("p (g t) -> p g t", g=3)
                                ).then_inc(is_freed(key)[0], 1)

            def row_max(G):
                n, U, key = G // 4, len(heads_of(G)), ("scores", G)
                S = bank_of(key)[:, 0:U * P].rearrange("p (u k) -> p u k", u=U)
                if G >= 2:
                    dve.wait_ge(*is_filled(("probs_turn", G - 2)))
                dve.wait_ge(*is_filled(key))
                if layer_of(n) == 0:
                    dve.tensor_tensor(z[:, G % 2, :, :], S, bias_mask[:, :].unsqueeze(1).to_broadcast([P, U, P]),
                                      ALU.add).then_inc(is_freed(key)[0], 1)
                    dve.wait_ge(*is_freed(key))
                    dve.tensor_reduce(neg_max[:, G % 2, 0:U], z[:, G % 2, :, :], AX_X, ALU.max,
                                      negate=True).then_inc(max_ready, 1)
                else:
                    dve.tensor_reduce(neg_max[:, G % 2, 0:U], S, AX_X, ALU.max, negate=True).then_inc(max_raw, 1)
                    dve.wait_ge(max_raw, 4 * ord1(n) + G % 4 + 1)
                    dve.tensor_scalar(neg_max_s[:, G % 2, 0:U], neg_max[:, G % 2, 0:U], SCORE_SCALE1, None,
                                      ALU.mult).then_inc(max_ready, 1)

            def row_inverse(G):
                U, key = len(heads_of(G)), ("scores", G)
                dve.wait_ge(exp_ready, G + 1)
                if layer_of(G // 4) == 1:
                    dve.sem_inc(is_freed(key)[0], 1)
                dve.reciprocal(row_inv[:, G % 2, 0:U], row_sum[:, G % 2, 0:U]).then_inc(inv_ready, 1)

            def residual(kind, n):
                key = ("project" if kind == "a" else "down", n)
                m, s, o = NM[kind], seq_of(n), ord0(n)
                dve.wait_ge(*is_filled(key))
                if layer_of(n) == 1:
                    dve.tensor_tensor(X[:, s, :], bank_of(key)[:, 0:C], X[:, s, :], ALU.add
                                      ).then_inc(is_freed(key)[0], 1)
                    return
                pair = ROUNDS[n // 2][0]
                dve.tensor_tensor(res_t[:, m, 0, :], bank_of(key)[:, 0:C], res_bias[:, m, :], ALU.add
                                  ).then_inc(is_freed(key)[0], 1)
                dve.wait_ge(*is_freed(key))
                dve.wait_ge(gamma_loaded[pair], 32)
                if o >= 1:
                    dve.wait_ge(res_ready[kind], o)
                dve.tensor_tensor(res_t[:, m, 1, :], res_t[:, m, 0, :], gamma[:, pair % 2, n % 2, m * C:(m + 1) * C],
                                  ALU.mult).then_inc(res_scaled[kind], 1)

            def gelu_inner(r, c):
                o = fc_ord(r, c)
                dve.wait_ge(g_poly, o + 1)
                dve.tensor_tensor(g_a[:, o % 2, :], g_b[:, o % 2, :], g_u[:, o % 2, :], ALU.mult
                                  ).then_inc(g_inner, 1)

            def gelu(r, c):
                o, m = fc_ord(r, c), mlp_ord(r, c)
                dve.wait_ge(g_tanh, m + 1)
                if c == 0 and r >= 1:
                    dve.wait_ge(*is_filled(("down", 2 * r - 1)))
                dve.scalar_tensor_tensor(out=g_h[:, 2 * c:2 * c + 2, :].rearrange("p f t -> p (f t)"),
                                         in0=g_a[:, o % 2, :], scalar=1.0, in1=g_u[:, o % 2, :],
                                         op0=ALU.add, op1=ALU.mult).then_inc(g_ready, 1)

            def gate(r, f):
                m, key = mlp_ord(r, f), ("gate_up", r, f)
                dve.wait_ge(g_tanh, m + 1)
                dve.scalar_tensor_tensor(out=g_b[:, f % 2, 0:256], in0=g_a[:, f % 2, 0:256], scalar=1.0,
                                         in1=bank_of(key)[:, 0:256], op0=ALU.add, op1=ALU.mult).then_inc(g_gated, 1)
                dve.wait_ge(g_gated, gu_ord(r, f) + 1)
                if f == 0 and r >= 1:
                    dve.wait_ge(*is_filled(("down", 2 * r - 1)))
                dve.scalar_tensor_tensor(out=g_h[:, f, :], in0=g_b[:, f % 2, 0:256], scalar=0.5,
                                         in1=bank_of(key)[:, 256:512], op0=ALU.mult, op1=ALU.mult
                                         ).then_inc(g_ready, 1)
                dve.wait_ge(g_ready, m + 1)
                dve.sem_inc(is_freed(key)[0], 1)

            steps = {"cond_silu": cond_silu_, "cond_copy": cond_copy, "angles": angles, "weight_low": weight_low,
                     "modulated": modulated, "norm_stats": norm_stats, "norm_apply": norm_apply,
                     "norm_mod": norm_mod, "qk_copy": qk_copy, "v_copy": v_copy, "qk_sum": qk_sum,
                     "qk_scale": qk_scale, "qk_low": qk_low_, "q_copy": q_copy, "k_copy": k_copy, "rope": rope,
                     "qk1_copy": qk1_copy, "row_max": row_max, "row_inverse": row_inverse, "residual": residual,
                     "gelu_inner": gelu_inner, "gelu": gelu, "gate": gate}
            for name, *a in ORDER["DVE"]:
                steps[name](*a)

        @block.tensor
        def _(pe):
            def take(key):
                b, t = PLAN[key]
                if t >= 1:
                    pe.wait_ge(freed[b], t)
                return psum[b], filled[b]

            def product3(dst, parts):
                last = len(parts) - 1
                for i, (sh, sl, mh, ml) in enumerate(parts):
                    pe.matmul(dst, sh, mh, start=i == 0, stop=False)
                    pe.matmul(dst, sh, ml, start=False, stop=False)
                    ins = pe.matmul(dst, sl, mh, start=False, stop=i == last)
                return ins

            def cond_turn():
                bank, full = take(("cond_turn",))
                pe.wait_ge(consts_set, 1)
                pe.wait_ge(vec_loaded, 16 * 5)
                pe.wait_ge(cond_silu, 1)
                for s, src in enumerate((silu8, cond8)):
                    for ct in range(CT):
                        at = (s * CT + ct) * N_SEQ
                        pe.transpose(bank[:, at:at + N_SEQ], src[:, ct * P:(ct + 1) * P], ident[0:N_SEQ, 0:N_SEQ])
                pe.transpose(bank[:, V0:V0 + N_VEC], vec_rows[:, :], ident[0:N_VEC, 0:N_VEC]).then_inc(full, 1)

            def weight_turn(c):
                name, i = CHUNKS[c]
                bank, full = take(("weight_turn", c))
                if c == 0:
                    pe.wait_ge(consts_set, 1)
                extra = sum(1 for q in range(c % STAGE, c + 1, STAGE) if CHUNKS[q][0] == "Wkv")
                pe.wait_ge(stage_loaded[c % STAGE], 16 * (c // STAGE + 1 + extra))
                raw = stage[:, c % STAGE, :]
                if name == "Wkv":
                    for ct in range(CT):
                        ins = pe.transpose(bank[:, ct * 2 * D1:(ct + 1) * 2 * D1],
                                           raw[0:2 * D1, ct * P:(ct + 1) * P], ident[0:2 * D1, 0:2 * D1])
                elif name in WIDE:
                    for ct in range(4):
                        ins = pe.transpose(bank[:, ct * P:(ct + 1) * P], raw[:, ct * P:(ct + 1) * P], ident[:, :])
                else:
                    for ct in range(CT):
                        for rt in range(2):
                            ins = pe.transpose(bank[:, (2 * ct + rt) * P:(2 * ct + rt + 1) * P],
                                               raw[:, rt * C + ct * P:rt * C + (ct + 1) * P], ident[:, :])
                ins.then_inc(full, 1)

            def modulate(c):
                chunk, o = CHUNKS[c], IS_ADA[c]
                bank, full = take(("modulate", c))
                pe.wait_ge(*is_freed(("weight_turn", c)))
                pe.wait_ge(*is_freed(("cond_turn",)))
                wt = adaT[:, o % 2, :, :]
                base = 0 if chunk[0] == "ada" else CT * N_SEQ
                cT = [cols[:, base + ct * N_SEQ:base + (ct + 1) * N_SEQ] for ct in range(CT)]
                if chunk[0] == "ada" and chunk[1] < 2:
                    for ct in range(CT):
                        ins = pe.matmul(bank[0:N_SEQ, 0:C], cT[ct], wt[:, ct, :], start=(ct == 0),
                                        stop=(ct == CT - 1))
                else:
                    for ft in range(CT):
                        for ct in range(CT):
                            ins = pe.matmul(bank[:, ft * N_SEQ:(ft + 1) * N_SEQ], wt[:, ct, ft * P:(ft + 1) * P],
                                            cT[ct], start=(ct == 0), stop=(ct == CT - 1))
                ins.then_inc(full, 1)

            def norm_turn(kind, n):
                bank, full = take(("norm_turn", kind, n))
                pe.wait_ge(xn_ready[kind], n + 1)
                for ft in range(CT):
                    ins = pe.transpose(bank[:, ft * P:(ft + 1) * P], xn[:, NM[kind], n % 2, ft * P:(ft + 1) * P],
                                       ident[:, :])
                ins.then_inc(full, 1)

            def token_major(key, n, wname, lo_col, width):
                bank, full = take(key)
                j = n % 2
                hi, lo = WT[wname]
                parts = [(h_hi[:, 0, ct, j * P:(j + 1) * P], h_lo[:, 0, ct, j * P:(j + 1) * P],
                          hi[:, ct, lo_col:lo_col + width], lo[:, ct, lo_col:lo_col + width]) for ct in range(CT)]
                return product3(bank[:, 0:width], parts), full

            def qk_product(n):
                pe.wait_ge(h_low["a"], n + 1)
                if n == 0:
                    for c in range(CHUNK_AT[("Wqkv", 0)], LAST_CHUNK["Wqkv"] + 1):
                        pe.wait_ge(*is_freed(("weight_turn", c)))
                ins, full = token_major(("qk_product", n), n, "Wqkv", 0, 2 * C)
                ins.then_inc(full, 1)

            def v_product(n):
                ins, full = token_major(("v_product", n), n, "Wqkv", 2 * C, C)
                ins.then_inc(full, 1)

            def qkv1_product(n):
                pe.wait_ge(h_low["a"], n + 1)
                for name in ("Wq", "Wkv"):
                    pe.wait_ge(*is_freed(("weight_turn", CHUNK_AT[(name, 0)])))
                ins, full = token_major(("qkv1_product", n), n, "Wqkv1", 0, QKV1)
                ins.then_inc(full, 1)

            def q_or_k_turn(key, slabs, n):
                bank, full = take((key, n))
                v = bank[:, :].bitcast(F16)
                for i, s in enumerate(slabs):
                    for g in range(4):
                        at = i * 512 + g * P
                        ins = pe.transpose(v[:, at:at + P],
                                           qk_pack[:, n % 2, s, 4 * g:4 * g + 4, :].rearrange("p h d -> p (h d)"),
                                           ident16[:, :])
                ins.then_inc(full, 1)

            def q_turn(n):
                pe.wait_ge(qk_packed, ord0(n) + 1)
                pe.wait_ge(consts_set, 2)
                q_or_k_turn("q_turn", (0, 2), n)

            def k_turn(n):
                q_or_k_turn("k_turn", (1,), n)

            def qk1_turn(n):
                pe.wait_ge(rope_ready, ord1(n) + 1)
                bank, full = take(("qk1_turn", n))
                for g in range(3):
                    ins = pe.transpose(bank[:, g * P:(g + 1) * P],
                                       qk1_rot[:, n % 2, 4 * g:4 * g + 4, :].rearrange("p h d -> p (h d)"),
                                       ident[:, :])
                ins.then_inc(full, 1)

            def scores(G):
                n, i, j = G // 4, G % 4, (G // 4) % 2
                bank, full = take(("scores", G))
                rows = slice(QUAD * i, QUAD * (i + 1))
                if i == 0:
                    if layer_of(n) == 0:
                        pe.wait_ge(*is_freed(("q_turn", n)))
                        pe.wait_ge(*is_freed(("k_turn", n)))
                    else:
                        pe.wait_ge(*is_freed(("qk1_turn", n)))
                for u, h in enumerate(heads_of(G)):
                    dst, g = bank[:, u * P:(u + 1) * P], h // 4
                    if layer_of(n) == 0:
                        pe.matmul(dst, qkT[rows, j, 0, g, :], qkT[rows, j, 1, g, :], start=True, stop=False)
                        ins = pe.matmul(dst, qkT[rows, j, 2, g, :], qkT[rows, j, 1, g, :], start=False, stop=True)
                    else:
                        ins = pe.matmul(dst, qk1T[rows, j, g, :], qk1T[rows, j, 2, :], start=True, stop=True)
                ins.then_inc(full, 1)

            def probs_turn(G):
                bank, full = take(("probs_turn", G))
                pe.wait_ge(probs_ready, G + 1)
                for u in range(len(heads_of(G))):
                    ins = pe.transpose(bank[:, u * P:(u + 1) * P], z[:, G % 2, u, :], ident[:, :])
                ins.then_inc(full, 1)

            def values(G):
                n, i, j = G // 4, G % 4, (G // 4) % 2
                b, t = PLAN[("values", 4 * n)]
                bank = psum[b]
                if i == 0 and t >= 1:
                    pe.wait_ge(freed[b], t)
                if i == 0 and layer_of(n) == 0:
                    pe.wait_ge(*is_freed(("v_product", n)))
                pe.wait_ge(*is_freed(("probs_turn", G)))
                for u, h in enumerate(heads_of(G)):
                    if layer_of(n) == 0:
                        tile, quad, even = h // 8, (h % 8) // 2, h % 2 == 0
                        stat = v_pad[:, j, h, :]
                        fresh, done = even and tile == 0, not even
                    else:
                        tile, quad = h // 4, h % 4
                        stat = qkv1[:, j, C + D1:QKV1]
                        fresh, done = tile == 0, True
                    rows = slice(QUAD * quad, QUAD * (quad + 1))
                    ins = pe.matmul(bank[rows, tile * P:(tile + 1) * P], stat, probsT[:, G % 2, u, :], start=fresh,
                                    stop=done, skip_group_check=True)
                ins.then_inc(values_summed, 1)

            def project(n):
                bank, full = take(("project", n))
                pe.wait_ge(*is_freed(("values", 4 * n)))
                name = "Wproj" if layer_of(n) == 0 else "Wo"
                pe.wait_ge(*is_freed(("weight_turn", LAST_CHUNK[name])))
                for ct in range(CT):
                    ins = pe.matmul(bank[:, 0:C], o_full[:, n % 2, ct, :], WT1[name][:, ct, :], start=(ct == 0),
                                    stop=(ct == CT - 1))
                ins.then_inc(full, 1)

            def hidden(key, names, tiles):
                bank, full = take(key)
                for s, (name, f) in enumerate(zip(names, tiles)):
                    hi, lo = WT[name]
                    ins = product3(bank[:, s * 256:(s + 1) * 256],
                                   [(hi[:, ct, f * P:(f + 1) * P], lo[:, ct, f * P:(f + 1) * P],
                                     h_hi[:, 1, ct, :], h_lo[:, 1, ct, :]) for ct in range(CT)])
                ins.then_inc(full, 1)

            def fc1(r, c):
                pe.wait_ge(h_low["m"], 2 * r + 2)
                pe.wait_ge(*is_freed(("weight_turn", CHUNK_AT[("Wfc1", 2 * c)])))
                hidden(("fc1", r, c), ("Wfc1", "Wfc1"), (2 * c, 2 * c + 1))

            def gate_up(r, f):
                pe.wait_ge(h_low["m"], 2 * r + 2)
                for name in ("Wg", "Wu"):
                    pe.wait_ge(*is_freed(("weight_turn", CHUNK_AT[(name, 2 * (f // 2))])))
                hidden(("gate_up", r, f), ("Wg", "Wu"), (f, f))

            def down(n):
                j, r = n % 2, n // 2
                bank, full = take(("down", n))
                name = "Wfc2" if layer_of(n) == 0 else "Wd"
                for c in range(CHUNK_AT[(name, 0)], LAST_CHUNK[name] + 1):
                    pe.wait_ge(*is_freed(("weight_turn", c)))
                pe.wait_ge(g_ready, mlp_ord(r + 1, 0))
                for f in range(FT):
                    ins = pe.matmul(bank[:, 0:C], g_h[:, f, j * P:(j + 1) * P], WT1[name][:, f, :],
                                    start=(f == 0), stop=(f == FT - 1))
                ins.then_inc(full, 1)

            steps = {"cond_turn": cond_turn, "weight_turn": weight_turn, "modulate": modulate,
                     "norm_turn": norm_turn, "qk_product": qk_product, "v_product": v_product,
                     "qkv1_product": qkv1_product, "q_turn": q_turn, "k_turn": k_turn, "qk1_turn": qk1_turn,
                     "scores": scores, "probs_turn": probs_turn, "values": values, "project": project,
                     "fc1": fc1, "gate_up": gate_up, "down": down}
            for name, *a in ORDER["PE"]:
                steps[name](*a)


NAMES = {"Wqkv": "L0_cond_Wqkv", "q_bias": "L0_cond_q_bias", "v_bias": "L0_cond_v_bias",
         "sml": "L0_cond_scale_mul_log", "Wproj": "L0_cond_Wproj", "bproj": "L0_cond_bproj",
         "Wada": "L0_cond_Wada", "bada": "L0_cond_bada", "Wfc1": "L0_cond_Wfc1", "bfc1": "L0_cond_bfc1",
         "Wfc2": "L0_cond_Wfc2", "bfc2": "L0_cond_bfc2", "ln1_w": "L1_cond_ln1_w", "tw1": "L1_cond_ln1_tw",
         "ln2_w": "L1_cond_ln2_w", "tw2": "L1_cond_ln2_tw", "Wq": "L1_cond_Wq", "Wk": "L1_cond_Wk",
         "Wv": "L1_cond_Wv", "Wo": "L1_cond_Wo", "Wg": "L1_cond_Wg", "Wu": "L1_cond_Wu", "Wd": "L1_cond_Wd"}


def kernel(**inputs):
    import numpy as _np
    import concourse.bacc as _bacc
    from concourse import mybir as _mybir
    from concourse.bass_utils import run_bass_kernel_spmd as _run

    nc = _bacc.Bacc("TRN2", target_bir_lowering=False, num_devices=1)
    arrays = {}

    def declare(name, shape=None, turned=False):
        a = _np.asarray(inputs[name])
        a = _np.ascontiguousarray(a.T if turned else a)
        if shape is not None:
            a = a.reshape(shape)
        arrays[f"in_{name}"] = a
        return nc.dram_tensor(f"in_{name}", a.shape, _mybir.dt.from_np(a.dtype), kind="ExternalInput").ap()

    x = declare("x")
    cond = declare("cond_2048")
    pos = declare("pos_BxS", turned=True)
    mask = declare("mask_1x1xSxS_ff0", (P, P))
    w = {k: declare(v, (H0,) if k == "sml" else None) for k, v in NAMES.items()}
    out = nc.dram_tensor("out", (N_SEQ, P, C), _mybir.dt.float32, kind="ExternalOutput").ap()
    build(nc, x, cond, pos, mask, w, out)
    r = _run(nc, [arrays], core_ids=[0])
    return r.results[0]["out"]
```
